# Optimizing a Trainium2 kernel written in Bass

```python
import numpy as np
import jax
import jax.numpy as jnp

def _softmax(x, axis=-1):
    return jax.nn.softmax(x, axis=axis)

def _gelu(x):
    return jax.nn.gelu(x, approximate=True)

def _silu(x):
    return jax.nn.silu(x)

def _sigmoid(x):
    return jax.nn.sigmoid(x)

def _layernorm(x, axis=-1, eps=1e-05):
    m = jnp.mean(x, axis=axis, keepdims=True)
    v = jnp.var(x, axis=axis, keepdims=True)
    return (x - m) / jnp.sqrt(v + eps)

def _scatter_add(tgt, idx, src, axis=0):
    return tgt.at[idx].add(src)

def _segment_sum(src, seg, n):
    return jax.ops.segment_sum(src, seg, n)
kernel_name = 'mk_sandwich_d1_jaxref_r4_b3492b'

def setup_inputs(seed: int=0):
    np.random.seed(seed)
    _w = jnp.asarray

    def _L0_attn_setup():
        import jax, jax.numpy as jnp
        from jax import lax
        import numpy as np
        B, T, C = (8, 256, 256)
        H = 4 * C
        TAU, VTH, ATAN_ALPHA = (2.0, 1.0, 2.0)

        @jax.custom_vjp
        def spike(x):
            return (x >= 0).astype(x.dtype)

        def _spike_fwd(x):
            return ((x >= 0).astype(x.dtype), x)

        def _spike_bwd(x, g):
            sg = ATAN_ALPHA / (2.0 * (1.0 + (jnp.pi / 2.0 * ATAN_ALPHA * x) ** 2))
            return (g * sg,)
        spike.defvjp(_spike_fwd, _spike_bwd)

        def layer_norm(x, s, b, eps=1e-05):
            m = jnp.mean(x, -1, keepdims=True)
            v = jnp.var(x, -1, keepdims=True)
            return (x - m) * lax.rsqrt(v + eps) * s + b

        def time_shift(x):
            return jnp.pad(x, ((0, 0), (1, 0), (0, 0)))[:, :-1]

        def wkv(w_decay, u, k, v):
            W = -jnp.exp(w_decay)
            kT = jnp.swapaxes(k, 0, 1)
            vT = jnp.swapaxes(v, 0, 1)
            p0 = jnp.zeros_like(kT[0])
            q0 = jnp.zeros_like(kT[0])
            o0 = jnp.full_like(kT[0], -1e+38)

            def step(carry, kv_t):
                p, q, o = carry
                kt, vt = kv_t
                no = jnp.maximum(o, u + kt)
                A = jnp.exp(o - no)
                Bc = jnp.exp(u + kt - no)
                y = (A * p + Bc * vt) / (A * q + Bc)
                no2 = jnp.maximum(W + o, kt)
                A2 = jnp.exp(W + o - no2)
                B2 = jnp.exp(kt - no2)
                return ((A2 * p + B2 * vt, A2 * q + B2, no2), y)
            _, ys = lax.scan(step, (p0, q0, o0), (kT, vT))
            return jnp.swapaxes(ys, 0, 1)

        def lif(x):
            xT = jnp.swapaxes(x, 0, 1)

            def step(v, xt):
                v = v + (xt - v) / TAU
                s = spike(v - VTH)
                return (v * (1.0 - s), s)
            _, sT = lax.scan(step, jnp.zeros_like(xT[0]), xT)
            return jnp.swapaxes(sT, 0, 1)

        def time_mix(x, tmk, tmv, tmr, w_decay, u_first, Wk, Wv, Wr, Wo):
            xx = time_shift(x)
            xk = x * tmk + xx * (1.0 - tmk)
            xv = x * tmv + xx * (1.0 - tmv)
            xr = x * tmr + xx * (1.0 - tmr)
            k = xk @ Wk
            v = xv @ Wv
            sr = jax.nn.sigmoid(xr @ Wr)
            return sr * wkv(w_decay, u_first, k, v) @ Wo

        def channel_mix(x, tmk, tmr, Wk, Wr, Wv):
            xx = time_shift(x)
            xk = x * tmk + xx * (1.0 - tmk)
            xr = x * tmr + xx * (1.0 - tmr)
            k = jnp.square(jax.nn.relu(xk @ Wk))
            return jax.nn.sigmoid(xr @ Wr) * (k @ Wv)
        key = jax.random.key(seed)
        ks = jax.random.split(key, 20)
        rn = lambda i, shape, s=1.0: s * jax.random.normal(ks[i], shape, dtype=jnp.float32)
        ru = lambda i, shape: jax.random.uniform(ks[i], shape, dtype=jnp.float32)
        return dict(x=rn(0, (B, T, C)), ln1_s=jnp.ones((C,), jnp.float32), ln1_b=jnp.zeros((C,), jnp.float32), ln2_s=jnp.ones((C,), jnp.float32), ln2_b=jnp.zeros((C,), jnp.float32), tmk=ru(1, (C,)), tmv=ru(2, (C,)), tmr=ru(3, (C,)), w_decay=rn(4, (C,), 0.5), u_first=rn(5, (C,), 0.5), Wk=rn(6, (C, C), 0.02), Wv=rn(7, (C, C), 0.02), Wr=rn(8, (C, C), 0.02), Wo=rn(9, (C, C), 0.02), f_tmk=ru(10, (C,)), f_tmr=ru(11, (C,)), fWk=rn(12, (C, H), 0.02), fWr=rn(13, (C, C), 0.02), fWv=rn(14, (H, C), 0.02))
    _L0_attn_in = _L0_attn_setup()

    def _L0_ffn_setup():
        import jax, jax.numpy as jnp
        import numpy as np
        BS, L, D = (4, 512, 256)
        H, E, K = (8, 16, 2)
        HD = D // H
        I = 1024 // H
        key = jax.random.key(seed)
        ks = jax.random.split(key, 10)
        s = lambda k, shp, fan: jax.random.normal(k, shp, jnp.float32) / np.sqrt(fan)
        return {'x': jax.random.normal(ks[0], (BS, L, D), jnp.float32), 'Wm': s(ks[1], (D, D), D), 'bm': jnp.zeros((D,), jnp.float32), 'expert_emb': jax.random.normal(ks[2], (HD, E), jnp.float32), 'W1': s(ks[3], (E, HD, I), HD), 'b1': jnp.zeros((E, I), jnp.float32), 'W2': s(ks[4], (E, I, HD), I), 'b2': jnp.zeros((E, HD), jnp.float32), 'Wo': s(ks[5], (D, D), D), 'bo': jnp.zeros((D,), jnp.float32)}
    _L0_ffn_in = _L0_ffn_setup()
    _d = {'L0_attn_x': _L0_attn_in['x'], 'L0_attn_ln1_s': _L0_attn_in['ln1_s'], 'L0_attn_ln1_b': _L0_attn_in['ln1_b'], 'L0_attn_ln2_s': _L0_attn_in['ln2_s'], 'L0_attn_ln2_b': _L0_attn_in['ln2_b'], 'L0_attn_tmk': _L0_attn_in['tmk'], 'L0_attn_tmv': _L0_attn_in['tmv'], 'L0_attn_tmr': _L0_attn_in['tmr'], 'L0_attn_w_decay': _L0_attn_in['w_decay'], 'L0_attn_u_first': _L0_attn_in['u_first'], 'L0_attn_Wk': _L0_attn_in['Wk'], 'L0_attn_Wv': _L0_attn_in['Wv'], 'L0_attn_Wr': _L0_attn_in['Wr'], 'L0_attn_Wo': _L0_attn_in['Wo'], 'L0_attn_f_tmk': _L0_attn_in['f_tmk'], 'L0_attn_f_tmr': _L0_attn_in['f_tmr'], 'L0_attn_fWk': _L0_attn_in['fWk'], 'L0_attn_fWr': _L0_attn_in['fWr'], 'L0_attn_fWv': _L0_attn_in['fWv'], 'L0_ffn_Wm': _L0_ffn_in['Wm'], 'L0_ffn_bm': _L0_ffn_in['bm'], 'L0_ffn_expert_emb': _L0_ffn_in['expert_emb'], 'L0_ffn_W1': _L0_ffn_in['W1'], 'L0_ffn_b1': _L0_ffn_in['b1'], 'L0_ffn_W2': _L0_ffn_in['W2'], 'L0_ffn_b2': _L0_ffn_in['b2'], 'L0_ffn_Wo': _L0_ffn_in['Wo'], 'L0_ffn_bo': _L0_ffn_in['bo']}
    _x0 = _d['L0_attn_x']
    _d['L0_attn_x'] = jax.random.normal(jax.random.fold_in(jax.random.key(seed), 1), (4, 2048, 256), dtype=_x0.dtype)
    del _x0
    return _d

def reference(L0_attn_x, L0_attn_ln1_s, L0_attn_ln1_b, L0_attn_ln2_s, L0_attn_ln2_b, L0_attn_tmk, L0_attn_tmv, L0_attn_tmr, L0_attn_w_decay, L0_attn_u_first, L0_attn_Wk, L0_attn_Wv, L0_attn_Wr, L0_attn_Wo, L0_attn_f_tmk, L0_attn_f_tmr, L0_attn_fWk, L0_attn_fWr, L0_attn_fWv, L0_ffn_Wm, L0_ffn_bm, L0_ffn_expert_emb, L0_ffn_W1, L0_ffn_b1, L0_ffn_W2, L0_ffn_b2, L0_ffn_Wo, L0_ffn_bo):

    def _L0_attn_ref(x, ln1_s, ln1_b, ln2_s, ln2_b, tmk, tmv, tmr, w_decay, u_first, Wk, Wv, Wr, Wo, f_tmk, f_tmr, fWk, fWr, fWv):
        import jax, jax.numpy as jnp
        from jax import lax
        import numpy as np
        B, T, C = (8, 256, 256)
        H = 4 * C
        TAU, VTH, ATAN_ALPHA = (2.0, 1.0, 2.0)

        @jax.custom_vjp
        def spike(x):
            return (x >= 0).astype(x.dtype)

        def _spike_fwd(x):
            return ((x >= 0).astype(x.dtype), x)

        def _spike_bwd(x, g):
            sg = ATAN_ALPHA / (2.0 * (1.0 + (jnp.pi / 2.0 * ATAN_ALPHA * x) ** 2))
            return (g * sg,)
        spike.defvjp(_spike_fwd, _spike_bwd)

        def layer_norm(x, s, b, eps=1e-05):
            m = jnp.mean(x, -1, keepdims=True)
            v = jnp.var(x, -1, keepdims=True)
            return (x - m) * lax.rsqrt(v + eps) * s + b

        def time_shift(x):
            return jnp.pad(x, ((0, 0), (1, 0), (0, 0)))[:, :-1]

        def wkv(w_decay, u, k, v):
            W = -jnp.exp(w_decay)
            kT = jnp.swapaxes(k, 0, 1)
            vT = jnp.swapaxes(v, 0, 1)
            p0 = jnp.zeros_like(kT[0])
            q0 = jnp.zeros_like(kT[0])
            o0 = jnp.full_like(kT[0], -1e+38)

            def step(carry, kv_t):
                p, q, o = carry
                kt, vt = kv_t
                no = jnp.maximum(o, u + kt)
                A = jnp.exp(o - no)
                Bc = jnp.exp(u + kt - no)
                y = (A * p + Bc * vt) / (A * q + Bc)
                no2 = jnp.maximum(W + o, kt)
                A2 = jnp.exp(W + o - no2)
                B2 = jnp.exp(kt - no2)
                return ((A2 * p + B2 * vt, A2 * q + B2, no2), y)
            _, ys = lax.scan(step, (p0, q0, o0), (kT, vT))
            return jnp.swapaxes(ys, 0, 1)

        def lif(x):
            xT = jnp.swapaxes(x, 0, 1)

            def step(v, xt):
                v = v + (xt - v) / TAU
                s = spike(v - VTH)
                return (v * (1.0 - s), s)
            _, sT = lax.scan(step, jnp.zeros_like(xT[0]), xT)
            return jnp.swapaxes(sT, 0, 1)

        def time_mix(x, tmk, tmv, tmr, w_decay, u_first, Wk, Wv, Wr, Wo):
            xx = time_shift(x)
            xk = x * tmk + xx * (1.0 - tmk)
            xv = x * tmv + xx * (1.0 - tmv)
            xr = x * tmr + xx * (1.0 - tmr)
            k = xk @ Wk
            v = xv @ Wv
            sr = jax.nn.sigmoid(xr @ Wr)
            return sr * wkv(w_decay, u_first, k, v) @ Wo

        def channel_mix(x, tmk, tmr, Wk, Wr, Wv):
            xx = time_shift(x)
            xk = x * tmk + xx * (1.0 - tmk)
            xr = x * tmr + xx * (1.0 - tmr)
            k = jnp.square(jax.nn.relu(xk @ Wk))
            return jax.nn.sigmoid(xr @ Wr) * (k @ Wv)
        x = x + lif(time_mix(layer_norm(x, ln1_s, ln1_b), tmk, tmv, tmr, w_decay, u_first, Wk, Wv, Wr, Wo))
        x = x + lif(channel_mix(layer_norm(x, ln2_s, ln2_b), f_tmk, f_tmr, fWk, fWr, fWv))
        return x

    def _L0_ffn_ref(x, Wm, bm, expert_emb, W1, b1, W2, b2, Wo, bo):
        import jax, jax.numpy as jnp
        import numpy as np
        BS, L, D = (4, 512, 256)
        H, E, K = (8, 16, 2)
        HD = D // H
        I = 1024 // H
        bs, L_, d = x.shape
        h = x @ Wm + bm
        t = h.reshape(bs * L_ * H, HD)
        logits = t @ expert_emb
        w = jax.nn.softmax(logits, axis=-1)
        topw, topi = jax.lax.top_k(w, K)
        hmid = jax.nn.gelu(jnp.einsum('td,edi->tei', t, W1) + b1, approximate=False)
        eo = jnp.einsum('tei,eio->teo', hmid, W2) + b2
        sel = jnp.take_along_axis(eo, topi[:, :, None], axis=1)
        comb = (sel * topw[:, :, None]).sum(axis=1)
        out = comb.reshape(bs, L_, d)
        return out @ Wo + bo
    x = L0_attn_x
    x = x + _layernorm(_L0_attn_ref(_layernorm(x, axis=-1), L0_attn_ln1_s, L0_attn_ln1_b, L0_attn_ln2_s, L0_attn_ln2_b, L0_attn_tmk, L0_attn_tmv, L0_attn_tmr, L0_attn_w_decay, L0_attn_u_first, L0_attn_Wk, L0_attn_Wv, L0_attn_Wr, L0_attn_Wo, L0_attn_f_tmk, L0_attn_f_tmr, L0_attn_fWk, L0_attn_fWr, L0_attn_fWv), axis=-1)
    x = x + _layernorm(_L0_ffn_ref(_layernorm(x, axis=-1), L0_ffn_Wm, L0_ffn_bm, L0_ffn_expert_emb, L0_ffn_W1, L0_ffn_b1, L0_ffn_W2, L0_ffn_b2, L0_ffn_Wo, L0_ffn_bo), axis=-1)
    return x

_drawn_inputs = setup_inputs


def setup_inputs(seed=0):
    import zlib

    import numpy as np

    out = dict(_drawn_inputs(seed))
    spreads = {'L0_attn_ln1_s': (1.0, 0.2),
     'L0_attn_ln1_b': (0.0, 0.1),
     'L0_attn_ln2_s': (1.0, 0.2),
     'L0_attn_ln2_b': (0.0, 0.1),
     'L0_ffn_bm': (0.0, 0.1),
     'L0_ffn_b1': (0.0, 0.1),
     'L0_ffn_b2': (0.0, 0.1),
     'L0_ffn_bo': (0.0, 0.1)}
    factors = {}
    for name, (base, spread) in spreads.items():
        noise = np.random.default_rng([zlib.crc32(name.encode()), seed]).standard_normal(out[name].shape)
        drawn = base * np.exp(spread * noise) if base else spread * noise
        out[name] = jnp.asarray(drawn.astype(out[name].dtype))
    for name, factor in factors.items():
        out[name] = (out[name] * factor).astype(out[name].dtype)
    return out
```

```python
from contextlib import ExitStack

import concourse.bass as bass
from concourse import mybir

F32 = mybir.dt.float32
F32R = mybir.dt.float32r
BF16 = mybir.dt.bfloat16
I32 = mybir.dt.int32
ALU = mybir.AluOpType
ACT = mybir.ActivationFunctionType
AX = mybir.AxisListType

P = 128
EPS = 1e-5
O_START = -1e38
FAR = -3e38
VTH = 1.0

STATS = 9
SMALL0, SMALL = 7, 2
MIX1, MIX2 = 6, 4
WKV = 22
LIF = 8
ROUTE = 20
SHIFT = 4


START = {"fin": 1, "ap3": 1, "cm_ps": 1, "acc_ok": 1, "x_out": 16}


class Steps:

    def __init__(self, eng, sem, n, per, start=0):
        self.eng, self.sem, self.base, self.per, self.k = eng, sem, n * per + start, per, 0

    def did(self, ins):
        ins.then_inc(self.sem, 1)
        self.k += 1

    def settle(self):
        self.eng.wait_ge(self.sem, self.base + self.k)

    def end(self):
        assert self.k == self.per, (self.k, self.per)
        self.settle()


def build(nc, a, out, chunks=None):
    x = a["L0_attn_x"]
    B, T, C = x.shape
    KB = C // P
    TC = P
    NCH = chunks or T // TC
    SEG = KB * B
    N = B * TC
    TS = TC + 1
    FB = a["L0_attn_fWk"].shape[1] // P
    H = 8
    E, HD, I = a["L0_ffn_W1"].shape
    NP = H // 2
    NG = 4
    EG = E // NG
    UNITS = NP * NG
    GS = 8
    assert HD * EG == P and I == P and KB == 2 and B == 4 and N == 512

    x_d = x.rearrange("b (n p) c -> n p b c", p=TC)
    out_d = out.rearrange("b (n p) c -> n p b c", p=TC)

    with ExitStack() as ctx:
        def sb(name, shape, dt=F32):
            return ctx.enter_context(nc.sbuf_tensor(name, shape, dt))

        def sem(name):
            return ctx.enter_context(nc.semaphore(name))

        wk, wv, wr, wo, fwr, fo = (sb(n, [P, KB, C]) for n in ("wk", "wv", "wr", "wo", "fwr", "fo"))
        fwk = sb("fwk", [P, KB, FB * P])
        fwv = sb("fwv", [P, FB, C])
        wm4 = sb("wm4", [P, KB, H, 4, HD])
        w1s = sb("w1s", [P, E, I], F32R)
        embs = sb("embs", [P, E], F32R)
        embf = sb("embf", [P, E])
        w2 = sb("w2", [P, E, HD])
        b1t = sb("b1t", [P, E])
        b2t = sb("b2t", [P, NG])
        bm4 = sb("bm4", [P, H])
        bo_b = sb("bo_b", [P, C])
        vecs = sb("vecs", [P, 11, KB])
        LN1S, LN1B, LN2S, LN2B, TMK, TMV, TMR, FTMK, FTMR, WDEC, UFIRST = range(11)
        wneg = sb("wneg", [P, KB])
        ident = sb("ident", [P, P])
        identb = sb("identb", [P, P], BF16)
        stack = sb("stack", [P, HD])
        pick = sb("pick", [P, 2, NG, P], BF16)
        desc = sb("desc", [P, E])
        decay = sb("decay", [P, SEG, TS])
        half = sb("half", [P, SEG, TS])
        nhalf = sb("nhalf", [P, B])

        eps4 = sb("eps4", [P, B])
        tick = sb("tick", [P, 2])

        last_a, last_c, last_o, last_p, last_q, last_v1, last_v2 = (
            sb(n, [P, SEG, 1]) for n in ("last_a", "last_c", "last_o", "last_p", "last_q", "last_v1", "last_v2"))

        xt = sb("xt", [P, B, C])
        res = sb("res", [P, B, C])
        nrm = sb("nrm", [P, B, C])
        xp = sb("xp", [P, B, C])
        z = sb("z", [P, B, C])
        stats = sb("stats", [P, B, 6])
        mv = sb("mv", [P, B, 2])
        tiny = sb("tiny", [P, 6, B])
        VE, RS, T0, T1, T2, R1 = range(6)
        rs01 = sb("rs01", [P, B])

        buf = [sb(f"buf{i}", [P, SEG, TS]) for i in range(11)]
        kk = sb("kk", [P, FB, N])
        y_t = sb("y_t", [P, KB, N])
        mxl = sb("mxl", [P, 1])
        fm = sb("fm", [1, 1])
        flag = sb("flag", [1, 1], I32)
        vtmp = sb("vtmp", [P, SEG, 1])

        ts = sb("ts", [P, H, N], F32R)
        g = [kk[:, 2 * i:2 * i + 2, :] for i in range(4)]
        g4 = sb("g4", [P, 4, 2, N])
        g = g + [g4[:, i] for i in range(4)]
        cw = sb("cw", [P, 2, 2, N])
        acc = sb("acc", [P, 2, 2, N])
        comb = y_t
        rt = sb("rt", [P, 4, B * H, E])
        wbs = rt[:, 0:2].rearrange("p i g e -> p i (g e)")
        rsm = sb("rsm", [P, 3, B * H])
        wb = sb("wb", [P, B * H, 4, E], BF16)
        wt = sb("wt", [P, NP, N], BF16)

        hp = [ctx.enter_context(nc.psum_tensor(f"hp{i}", [P, 2, N], F32)) for i in range(2)]
        rp = ctx.enter_context(nc.psum_tensor("rp", [P, 2, N], F32))
        mp = ctx.enter_context(nc.psum_tensor("mp", [P, 2, N], F32))
        mseg = mp[:, :, :].rearrange("p k (b t) -> p (k b) t", b=B)
        mtok = mp[:, :, :].rearrange("p k n -> p (k n)").rearrange("p (b c) -> p b c", b=B)
        mlog = mp[:, 0, :].rearrange("p (g e) -> p g e", e=E)
        mwt = mp[:, :, :].bitcast(BF16).rearrange("p k n -> p (k n)").rearrange("p (q n) -> p q n", q=NP)

        names = """w_in w_rest konst prep x_in st0 sm0 ap0 t1_ps a_t d1 mix1 k_ps kvr wkv pool_wkv act_wkv
        u_ps xh1 lif1 f1_ps s1_ps x1_ok st2 sm2 ap2 t2_ps c_t d2 mix2 r2_ps er2 fk_ps relu sq kv_ps gate
        lif2 f2_ps s2_ps x2_ok st3 sm3 ap3 st4 sm4 ap4 t4_ps y_ok pj_ps t_hi t_lo lg_ps route exps
        wt_ps wt_ok l1_ps g_ok l2_ps wb_ps wb_ok c_ok acc_ok cm_ps cm_ok o_ps fin st5 sm5 ap5 x_out slow"""
        s = {n: sem(n) for n in names.split()}
        block = ctx.enter_context(nc.Block())

        def cols(t):
            return t[:, :, 1:TS]

        def before(t):
            return t[:, :, 0:TC]

        def blk(t, k):
            return t[:, k * B:(k + 1) * B, :]

        def vec(i, k):
            return vecs[:, i, k:k + 1]

        AT, D, XK, XV, XR = buf[0], buf[1], buf[2], buf[3], buf[4]
        K, V, ER = buf[5], buf[6], buf[7]
        O, A2, B2, BV, PS, QS, DD, AB, NUM, DEN, Y, TV = (
            buf[0], buf[1], buf[2], buf[3], buf[8], buf[9], buf[4], buf[10], buf[5], buf[1], buf[0], buf[2])
        XH, WL, S = buf[8], buf[9], buf[10]

        def dense(t):
            flat = t[:, :, :].rearrange("p s t -> p (s t)")
            return flat[:, 0:KB * N].rearrange("p (k n) -> p k n", k=KB)

        def seg(t):
            return dense(t).rearrange("p k (b t) -> p (k b) t", b=B)

        w1raw_all = kk[:, 0:4, :].rearrange("p f n -> p (f n)").rearrange("p (e i) -> p e i", e=E)

        def w1raw(q):
            return w1raw_all[q, :, :]

        wmraw = z[:, 0:KB, :]
        W_ALL = 16 * (11 + 8 + 4 * 4 + 4)
        KONST = 10 + E + 7 + 1 + 2 + 4 + 2 * NG * 3 + 4
        W_REST = 2 + 4 + KB + 1

        @block.sync
        def _(sp):
            sp.sem_inc(s["x_out"], START["x_out"])
            count = [0]

            def load(dst, src):
                sp.dma_start(dst, src).then_inc(s["w_in"], 16)
                count[0] += 16

            with nc.allow_non_contiguous_dma(reason="small vectors"):
                for i, name in enumerate(("ln1_s", "ln1_b", "ln2_s", "ln2_b", "tmk", "tmv", "tmr", "f_tmk",
                                          "f_tmr", "w_decay", "u_first")):
                    load(vecs[:, i, :], a["L0_attn_" + name].rearrange("(k p) -> p k", p=P))
                for t, name in ((wk, "L0_attn_Wk"), (wv, "L0_attn_Wv"), (wr, "L0_attn_Wr"), (wo, "L0_attn_Wo"),
                                (fwr, "L0_attn_fWr"), (fo, "L0_ffn_Wo"), (fwk, "L0_attn_fWk"),
                                (fwv, "L0_attn_fWv")):
                    load(t[:, :, :], a[name].rearrange("(k p) m -> p k m", p=P))
                for r in range(4):
                    q = slice(HD * r, HD * r + HD)
                    load(w1raw(q), a["L0_ffn_W1"].rearrange("e d i -> d e i"))
                    load(embf[q, :], a["L0_ffn_expert_emb"])
                    load(bm4[q, :], a["L0_ffn_bm"].rearrange("(h i) -> i h", i=HD))
                    load(b2t[q, :], a["L0_ffn_b2"].rearrange("(g j) o -> j o g", j=EG)[r])
                load(wmraw, a["L0_ffn_Wm"].rearrange("(k p) m -> p k m", p=P))
                load(w2[:, :, :], a["L0_ffn_W2"].rearrange("e i o -> i e o"))
                load(b1t[:, :], a["L0_ffn_b1"].rearrange("e i -> i e"))
                load(bo_b[:, :], a["L0_ffn_bo"].rearrange("(o c) -> o c", o=1).to_broadcast([P, C]))
            assert count[0] == W_ALL, count[0]

            def step(n, later):
                sp.wait_ge(s["ap3"], START["ap3"] + n * 5)
                sp.dma_start(xt[:, :, :], x_d[n]).then_inc(s["x_in"], 16)

            with sp.Fori(0, NCH) as n:
                step(n, True)
                sp.wait_ge(s["ap5"], n * 5 + 5)
                sp.dma_start(out_d[n], z[:, :, :]).then_inc(s["x_out"], 16)
            sp.wait_ge(s["x_out"], START["x_out"] + NCH * 16)

        @block.gpsimd
        def _(pool):
            pl = nc.gpsimd
            pool.sem_inc(s["acc_ok"], START["acc_ok"])
            k = [0]

            def did(ins):
                ins.then_inc(s["konst"], 1)
                k[0] += 1

            def settle():
                pool.wait_ge(s["konst"], k[0])

            for t in (ident, identb, stack):
                did(pl.memset(t[:, :], 0.0))
            did(pl.memset(pick[:, :, :, :], 0.0))
            did(pl.memset(nhalf[:, :], -0.5))
            did(pl.memset(eps4[:, :], EPS))
            did(pl.memset(tick[:, :], 0.0))
            did(pl.memset(half[:, :, :], 0.5))
            did(pl.memset(decay[:, :, :], 0.0))
            did(pl.memset(wb[:, :, :, :], 0.0))
            for e in range(E):
                did(pl.memset(desc[:, e:e + 1], float(E - e)))
            for t in (last_a, last_c, last_p, last_q, last_v1, last_v2):
                did(pl.memset(t[:, :, :], 0.0))
            did(pl.memset(last_o[:, :, :], O_START))
            settle()
            did(pl.memset(half[:, :, 0:1], 0.0))
            for t in (ident, identb):
                did(pl.affine_select(out=t[:, :], in_=t[:, :], compare_op=ALU.not_equal, fill=1.0, base=0,
                                     pattern=[[-1, P]], channel_multiplier=1))
            for r in range(4):
                settle()
                did(pl.affine_select(out=stack[:, :], in_=stack[:, :], compare_op=ALU.not_equal, fill=1.0,
                                     base=-HD * r, pattern=[[-1, HD]], channel_multiplier=1))
            for hh in range(2):
                for gg in range(NG):
                    for part in range(3):
                        settle()
                        v = pick[:, hh, gg, :].rearrange("p (j o) -> p j o", j=EG)
                        did(pl.affine_select(out=v, in_=v, compare_op=ALU.not_equal, fill=1.0,
                                             base=-(64 * hh + E * part + EG * gg),
                                             pattern=[[-1, EG], [0, HD]], channel_multiplier=1))
            pool.wait_ge(s["w_in"], W_ALL)
            for r in range(4):
                did(pl.tensor_copy(wm4[:, :, :, r, :], wmraw.rearrange("p k (h i) -> p k h i", i=HD)))
            settle()
            assert k[0] == KONST, k[0]

            def roots(st, sm, n, per, tail=False):
                q = Steps(pool, s[sm], n, per)
                pool.wait_ge(s[st], n * STATS + STATS)
                q.did(pl.tensor_tensor(tiny[:, VE, :], mv[:, :, 1], eps4[:, :], ALU.add))
                q.settle()
                q.did(pl.tensor_tensor(tiny[:, RS, :], tiny[:, VE, :], nhalf[:, :], ALU.pow))
                if tail:
                    q.settle()
                    q.did(pl.tensor_tensor(tiny[:, T0, :], mv[:, :, 1], tiny[:, RS, :], ALU.mult))
                    q.settle()
                    q.did(pl.tensor_tensor(tiny[:, T1, :], tiny[:, T0, :], tiny[:, RS, :], ALU.mult))
                    q.settle()
                    q.did(pl.tensor_tensor(tiny[:, T2, :], tiny[:, T1, :], eps4[:, :], ALU.add))
                    q.settle()
                    q.did(pl.tensor_tensor(tiny[:, R1, :], tiny[:, T2, :], nhalf[:, :], ALU.pow))
                    q.settle()
                    q.did(pl.tensor_tensor(rs01[:, :], tiny[:, RS, :], tiny[:, R1, :], ALU.mult))
                q.end()

            with pool.Fori(0, NCH) as n:
                roots("st0", "sm0", n, SMALL0, tail=True)
                pool.wait_ge(s["a_t"], n * SHIFT + SHIFT)
                pl.tensor_tensor(seg(D), cols(AT), before(AT), ALU.subtract).then_inc(s["d1"], 1)
                q = Steps(pool, s["pool_wkv"], n, 4)
                pool.wait_ge(s["wkv"], n * WKV + 2)
                q.did(pl.tensor_tensor(cols(B2), cols(K), cols(O), ALU.subtract))
                pool.wait_ge(s["act_wkv"], n * 4 + 2)
                q.did(pl.tensor_tensor(cols(BV), cols(B2), seg(V), ALU.mult))
                pool.wait_ge(s["act_wkv"], n * 4 + 4)
                pool.wait_ge(s["wkv"], n * WKV + 14)
                q.did(pl.tensor_tensor(seg(TV), seg(DD), seg(V), ALU.mult))
                q.did(pl.tensor_tensor(seg(DEN), seg(AB), before(QS), ALU.mult))
                q.end()
                roots("st2", "sm2", n, SMALL)
                pool.wait_ge(s["c_t"], n * SHIFT + SHIFT)
                pl.tensor_tensor(seg(D), cols(AT), before(AT), ALU.subtract).then_inc(s["d2"], 1)
                for r in range(4):
                    pool.wait_ge(s["relu"], n * 4 + r + 1)
                    v = kk[:, 2 * r:2 * r + 2, :]
                    pl.tensor_tensor(v, v, v, ALU.mult).then_inc(s["sq"], 1)
                roots("st3", "sm3", n, SMALL)
                roots("st4", "sm4", n, SMALL)
                q = Steps(pool, s["acc_ok"], n, NP * 3, START["acc_ok"])
                for p in range(NP):
                    for gg in range(1, NG):
                        u = NG * p + gg
                        pool.wait_ge(s["c_ok"], n * UNITS + u + 1)
                        if gg == 1:
                            pool.wait_ge(s["cm_ps"], START["cm_ps"] + n * NP + max(p - 1, 0))
                        old = cw[:, 0] if gg == 1 else acc[:, p % 2]
                        q.did(pl.tensor_tensor(acc[:, p % 2], old, cw[:, u % 2], ALU.add))
                        q.settle()
                q.end()
                roots("st5", "sm5", n, SMALL)

        @block.scalar
        def _(act):
            sc = nc.scalar
            act.wait_ge(s["w_in"], W_ALL)
            act.wait_ge(s["konst"], KONST)
            sc.activation(wneg[:, :], vecs[:, WDEC, :], ACT.Exp).then_inc(s["prep"], 1)
            act.wait_ge(s["prep"], 1)
            sc.mul(wneg[:, :], wneg[:, :], -1.0).then_inc(s["prep"], 1)

            def shifted(name, ps, last, sv, bv, n):
                q = Steps(act, s[name], n, SHIFT)
                act.wait_ge(s[ps], n + 1)
                q.did(sc.copy(AT[:, :, 0:1], last[:, :, :]))
                for k in range(KB):
                    q.did(sc.activation(cols(blk(AT, k)), mseg[:, k * B:(k + 1) * B, :], ACT.Identity,
                                        bias=vec(bv, k), scale=vec(sv, k)))
                q.settle()
                q.did(sc.copy(last[:, :, :], AT[:, :, TC:TS]))
                q.end()

            with act.Fori(0, NCH) as n:
                shifted("a_t", "t1_ps", last_a, LN1S, LN1B, n)
                q = Steps(act, s["kvr"], n, 3)
                act.wait_ge(s["k_ps"], n * 3 + 1)
                q.did(sc.copy(cols(K), mseg))
                act.wait_ge(s["k_ps"], n * 3 + 2)
                q.did(sc.copy(seg(V), mseg))
                act.wait_ge(s["k_ps"], n * 3 + 3)
                q.did(sc.activation(seg(ER), mseg, ACT.Exp, scale=-1.0))
                q.end()
                q = Steps(act, s["act_wkv"], n, 4)
                act.wait_ge(s["wkv"], n * WKV + 4)
                q.did(sc.activation(cols(A2), cols(A2), ACT.Exp))
                act.wait_ge(s["pool_wkv"], n * 4 + 1)
                q.did(sc.activation(cols(B2), cols(B2), ACT.Exp))
                act.wait_ge(s["wkv"], n * WKV + 9)
                q.did(sc.activation(seg(AB), seg(AB), ACT.Exp, scale=-1.0))
                q.did(sc.activation(seg(DD), seg(DD), ACT.Exp))
                q.end()
                act.wait_ge(s["u_ps"], n + 1)
                sc.mul(cols(XH), mseg, 0.5).then_inc(s["xh1"], 1)
                shifted("c_t", "t2_ps", last_c, LN2S, LN2B, n)
                act.wait_ge(s["r2_ps"], n + 1)
                sc.activation(seg(ER), mseg, ACT.Exp, scale=-1.0).then_inc(s["er2"], 1)
                for r in range(4):
                    act.wait_ge(s["fk_ps"], n * 4 + r + 1)
                    sc.activation(kk[:, 2 * r:2 * r + 2, :], mp[:, :, :], ACT.Relu).then_inc(s["relu"], 1)
                act.wait_ge(s["t4_ps"], n + 1)
                sc.copy(y_t[:, :, :], mp[:, :, :]).then_inc(s["y_ok"], 1)
                for h in range(H):
                    act.wait_ge(s["pj_ps"], n * NP + h // 2 + 1)
                    sc.activation(ts[:, h, :], mp[:, h % 2, :], ACT.Identity,
                                  bias=bm4[:, h:h + 1]).then_inc(s["t_hi"], 1)
                act.wait_ge(s["route"], n * ROUTE + 2)
                sc.activation(rt[:, 1], rt[:, 0], ACT.Exp).then_inc(s["exps"], 1)
                for i in range(UNITS * EG):
                    act.wait_ge(s["l1_ps"], n * UNITS * EG + i + 1)
                    u = i // EG
                    if u >= 2 and i % EG == 0:
                        act.wait_ge(s["l2_ps"], n * UNITS + u - 1)
                    e = i % E
                    sc.activation(g[i % GS], hp[i % 2][:, :, :], ACT.Gelu,
                                  bias=b1t[:, e:e + 1]).then_inc(s["g_ok"], 1)
                for c in range(2):
                    act.wait_ge(s["cm_ps"], START["cm_ps"] + n * NP + 2 * c + 2)
                    sc.copy(comb[:, c, :], mp[:, c, :]).then_inc(s["cm_ok"], 1)

        @block.vector
        def _(dve):
            ve = nc.vector
            dve.sem_inc(s["fin"], START["fin"])
            dve.sem_inc(s["ap3"], START["ap3"])
            dve.wait_ge(s["w_in"], W_ALL)
            dve.wait_ge(s["konst"], KONST)
            p = Steps(dve, s["w_rest"], 0, W_REST)
            p.did(ve.tensor_copy(w1s[:, :, :], w1raw(slice(0, P))))
            p.did(ve.tensor_copy(embs[:, :], embf[:, :]))
            p.settle()
            for r in (1, 3):
                q = slice(HD * r, HD * r + HD)
                p.did(ve.tensor_tensor(w1s[q, :, :], w1raw(q), w1s[q, :, :].bitcast(F32), ALU.subtract))
                p.did(ve.tensor_tensor(embs[q, :], embf[q, :], embs[q, :].bitcast(F32), ALU.subtract))
            dve.wait_ge(s["prep"], 2)
            for k in range(KB):
                p.did(ve.tensor_scalar(blk(decay, k), blk(decay, k), wneg[:, k:k + 1], None, ALU.add))
            p.settle()
            p.did(ve.memset(decay[:, :, 0:1], FAR))
            p.end()

            def held(q):
                q.did(ve.tensor_copy(tick[:, 1:2], tick[:, 0:1]))

            def layer_stats(name, src, n):
                q = Steps(dve, s[name], n, STATS)
                for j in range(B):
                    q.did(ve.bn_stats(stats[:, j, :], src[:, j, :]))
                q.settle()
                held(q)
                for j in range(B):
                    q.did(ve.bn_aggr(mv[:, j, :], stats[:, j, :]))
                q.end()

            def normalise(q, dst, src, rs):
                for j in range(B):
                    q.did(ve.tensor_scalar(dst[:, j, :], src[:, j, :], mv[:, j, 0:1], rs[:, j:j + 1],
                                           ALU.subtract, ALU.mult))

            def lif(name, ps, last, n):
                q = Steps(dve, s[name], n, LIF)
                q.did(ve.tensor_copy(XH[:, :, 0:1], last[:, :, :]))
                q.settle()
                flat = lambda t: t[:, :, :].rearrange("p s t -> p (s t)")
                q.did(ve.tensor_tensor_scan(flat(WL), flat(half), flat(XH), 0.0, ALU.mult, ALU.add))
                q.settle()
                q.did(ve.tensor_reduce(mxl[:, :], flat(WL), AX.X, ALU.max))
                dve.wait_ge(s[ps], n + 1)
                q.did(ve.tensor_reduce(fm[:, :], mp[0:1, 0, 0:P], AX.X, ALU.max))
                q.settle()
                q.did(ve.tensor_scalar(flag[:, :], fm[:, :], VTH, None, ALU.is_ge))
                q.settle()
                held(q)
                fires = dve.value_load(flag[0:1, 0:1], min_val=0, max_val=1)
                with dve.If(fires != 0):
                    q.settle()
                    ve.tensor_copy(tick[:, 1:2], tick[:, 0:1]).then_inc(s["slow"], 1)
                    with dve.Fori(1, TS) as t:
                        dve.wait_ge(s["slow"], 2 * t - 1)
                        ve.scalar_tensor_tensor(vtmp[:, :, :], WL[:, :, bass.ds(t - 1, 1)], VTH,
                                                WL[:, :, bass.ds(t - 1, 1)], ALU.is_lt,
                                                ALU.mult).then_inc(s["slow"], 1)
                        dve.wait_ge(s["slow"], 2 * t)
                        ve.scalar_tensor_tensor(WL[:, :, bass.ds(t, 1)], vtmp[:, :, :], 0.5,
                                                XH[:, :, bass.ds(t, 1)], ALU.mult,
                                                ALU.add).then_inc(s["slow"], 1)
                    dve.wait_ge(s["slow"], 2 * TC + 1)
                    dve.sem_clear(s["slow"])
                q.did(ve.tensor_scalar(seg(S), cols(WL), VTH, None, ALU.is_ge))
                q.did(ve.scalar_tensor_tensor(last[:, :, :], WL[:, :, TC:TS], VTH, WL[:, :, TC:TS],
                                              ALU.is_lt, ALU.mult))
                q.end()

            with dve.Fori(0, NCH) as n:
                dve.wait_ge(s["x_in"], n * 16 + 16)
                layer_stats("st0", xt, n)
                q = Steps(dve, s["ap0"], n, 8)
                dve.wait_ge(s["sm0"], n * SMALL0 + SMALL0)
                normalise(q, res, xt, tiny[:, RS, :])
                normalise(q, nrm, xt, rs01)
                q.end()
                q = Steps(dve, s["mix1"], n, MIX1)
                dve.wait_ge(s["d1"], n + 1)
                for dst, m in ((XK, TMK), (XV, TMV), (XR, TMR)):
                    for k in range(KB):
                        q.did(ve.scalar_tensor_tensor(blk(seg(dst), k), blk(seg(D), k), vec(m, k),
                                                      before(blk(AT, k)), ALU.mult, ALU.add))
                q.end()
                q = Steps(dve, s["wkv"], n, WKV)
                flat = lambda t: t[:, :, :].rearrange("p s t -> p (s t)")
                dve.wait_ge(s["kvr"], n * 3 + 3)
                q.did(ve.tensor_copy(K[:, :, 0:1], last_o[:, :, :]))
                q.settle()
                q.did(ve.tensor_tensor_scan(flat(O), flat(decay), flat(K), 0.0, ALU.add, ALU.max))
                q.settle()
                for k in range(KB):
                    q.did(ve.scalar_tensor_tensor(cols(blk(A2, k)), before(blk(O, k)), wneg[:, k:k + 1],
                                                  cols(blk(O, k)), ALU.add, ALU.subtract))
                for k in range(KB):
                    q.did(ve.scalar_tensor_tensor(blk(seg(DD), k), cols(blk(K, k)), vec(UFIRST, k),
                                                  before(blk(O, k)), ALU.add, ALU.subtract))
                q.did(ve.tensor_copy(last_o[:, :, :], O[:, :, TC:TS]))
                q.settle()
                q.did(ve.tensor_scalar(seg(AB), seg(DD), 0.0, None, ALU.max))
                q.settle()
                q.did(ve.tensor_scalar(seg(DD), seg(DD), 0.0, None, ALU.min))
                q.did(ve.memset(A2[:, :, 0:1], 0.0))
                q.did(ve.tensor_copy(BV[:, :, 0:1], last_p[:, :, :]))
                dve.wait_ge(s["pool_wkv"], n * 4 + 2)
                q.did(ve.tensor_copy(B2[:, :, 0:1], last_q[:, :, :]))
                dve.wait_ge(s["act_wkv"], n * 4 + 1)
                q.settle()
                q.did(ve.tensor_tensor_scan(flat(PS), flat(A2), flat(BV), 0.0, ALU.mult, ALU.add))
                q.did(ve.tensor_tensor_scan(flat(QS), flat(A2), flat(B2), 0.0, ALU.mult, ALU.add))
                q.settle()
                q.did(ve.tensor_copy(last_p[:, :, :], PS[:, :, TC:TS]))
                q.did(ve.tensor_copy(last_q[:, :, :], QS[:, :, TC:TS]))
                dve.wait_ge(s["act_wkv"], n * 4 + 4)
                q.did(ve.tensor_tensor(seg(NUM), seg(AB), before(PS), ALU.mult))
                q.settle()
                dve.wait_ge(s["pool_wkv"], n * 4 + 4)
                q.did(ve.tensor_tensor(seg(NUM), seg(NUM), seg(TV), ALU.add))
                q.did(ve.tensor_tensor(seg(DEN), seg(DEN), seg(DD), ALU.add))
                q.settle()
                q.did(ve.scalar_tensor_tensor(seg(DEN), seg(ER), 1.0, seg(DEN), ALU.add, ALU.mult))
                q.settle()
                q.did(ve.reciprocal(seg(DEN), seg(DEN)))
                q.settle()
                q.did(ve.tensor_tensor(seg(Y), seg(NUM), seg(DEN), ALU.mult))
                q.end()
                dve.wait_ge(s["xh1"], n + 1)
                lif("lif1", "f1_ps", last_v1, n)
                dve.wait_ge(s["s1_ps"], n + 1)
                ve.tensor_tensor(res[:, :, :], res[:, :, :], mtok, ALU.add).then_inc(s["x1_ok"], 1)
                dve.wait_ge(s["x1_ok"], n + 1)
                layer_stats("st2", res, n)
                q = Steps(dve, s["ap2"], n, 4)
                dve.wait_ge(s["sm2"], n * SMALL + SMALL)
                normalise(q, nrm, res, tiny[:, RS, :])
                q.end()
                q = Steps(dve, s["mix2"], n, MIX2)
                dve.wait_ge(s["d2"], n + 1)
                for dst, m in ((XR, FTMR), (XK, FTMK)):
                    for k in range(KB):
                        q.did(ve.scalar_tensor_tensor(blk(seg(dst), k), blk(seg(D), k), vec(m, k),
                                                      before(blk(AT, k)), ALU.mult, ALU.add))
                q.end()
                q = Steps(dve, s["gate"], n, 3)
                dve.wait_ge(s["er2"], n + 1)
                q.did(ve.tensor_scalar(seg(ER), seg(ER), 1.0, 2.0, ALU.add, ALU.mult))
                q.settle()
                q.did(ve.reciprocal(seg(ER), seg(ER)))
                q.settle()
                dve.wait_ge(s["kv_ps"], n + 1)
                q.did(ve.tensor_tensor(cols(XH), seg(ER), mseg, ALU.mult))
                q.end()
                lif("lif2", "f2_ps", last_v2, n)
                dve.wait_ge(s["s2_ps"], n + 1)
                ve.tensor_tensor(res[:, :, :], res[:, :, :], mtok, ALU.add).then_inc(s["x2_ok"], 1)
                dve.wait_ge(s["x2_ok"], n + 1)
                layer_stats("st3", res, n)
                q = Steps(dve, s["ap3"], n, 5, START["ap3"])
                dve.wait_ge(s["sm3"], n * SMALL + SMALL)
                normalise(q, nrm, res, tiny[:, RS, :])
                q.settle()
                q.did(ve.tensor_tensor(xp[:, :, :], nrm[:, :, :], xt[:, :, :], ALU.add))
                q.end()
                layer_stats("st4", xp, n)
                q = Steps(dve, s["ap4"], n, 4)
                dve.wait_ge(s["sm4"], n * SMALL + SMALL)
                normalise(q, nrm, xp, tiny[:, RS, :])
                q.end()
                for h in range(H):
                    dve.wait_ge(s["t_hi"], n * H + h // 2 * 2 + 2)
                    ve.scalar_tensor_tensor(ts[64:P, h, :], mp[64:P, h % 2, :], bm4[64:P, h:h + 1],
                                            ts[64:P, h, :].bitcast(F32), ALU.add,
                                            ALU.subtract).then_inc(s["t_lo"], 1)
                q = Steps(dve, s["route"], n, ROUTE)
                d, ex, hot, tmp = (rt[:, i] for i in range(4))
                mx = rsm[:, 0, :]

                def wide(v):
                    return v.rearrange("p (g o) -> p g o", o=1).to_broadcast([P, B * H, E])

                first = desc[:, :].rearrange("p (o e) -> p o e", o=1).to_broadcast([P, B * H, E])
                dve.wait_ge(s["lg_ps"], n + 1)
                q.did(ve.tensor_reduce(mx, mlog, AX.X, ALU.max))
                q.settle()
                q.did(ve.tensor_tensor(d, mlog, wide(mx), ALU.subtract))
                q.settle()
                q.did(ve.scalar_tensor_tensor(tmp, d, 0.0, first, ALU.is_equal, ALU.mult))
                q.settle()
                q.did(ve.tensor_reduce(mx, tmp, AX.X, ALU.max))
                q.settle()
                q.did(ve.tensor_tensor(hot, tmp, wide(mx), ALU.is_equal))
                q.settle()
                dve.wait_ge(s["exps"], n + 1)
                q.did(ve.scalar_tensor_tensor(d, hot, FAR, d, ALU.mult, ALU.add))
                q.settle()
                q.did(ve.tensor_reduce(mx, d, AX.X, ALU.max))
                q.settle()
                q.did(ve.tensor_tensor(d, d, wide(mx), ALU.subtract))
                q.settle()
                q.did(ve.scalar_tensor_tensor(tmp, d, 0.0, first, ALU.is_equal, ALU.mult))
                q.settle()
                q.did(ve.tensor_reduce(mx, tmp, AX.X, ALU.max))
                q.settle()
                q.did(ve.tensor_tensor(tmp, tmp, wide(mx), ALU.is_equal))
                q.settle()
                q.did(ve.tensor_tensor(hot, hot, tmp, ALU.add))
                q.did(ve.tensor_reduce(rsm[:, 1, :], ex, AX.X, ALU.add))
                q.settle()
                q.did(ve.reciprocal(rsm[:, 2, :], rsm[:, 1, :]))
                q.did(ve.tensor_tensor(hot, hot, ex, ALU.mult))
                q.settle()
                q.did(ve.tensor_tensor(hot, hot, wide(rsm[:, 2, :]), ALU.mult))
                q.settle()
                q.did(ve.tensor_copy(wb[:, :, 0, :], hot))
                q.settle()
                q.did(ve.tensor_tensor(tmp, hot, wb[:, :, 0, :], ALU.subtract))
                q.settle()
                q.did(ve.tensor_copy(wb[:, :, 1, :], tmp))
                q.settle()
                q.did(ve.tensor_tensor(wb[:, :, 2, :], tmp, wb[:, :, 1, :], ALU.subtract))
                q.end()
                dve.wait_ge(s["wt_ps"], n + 1)
                ve.tensor_copy(wt[:, :, :], mwt).then_inc(s["wt_ok"], 1)
                for u in range(UNITS):
                    dve.wait_ge(s["wb_ps"], n * UNITS + u + 1)
                    if u:
                        dve.wait_ge(s["c_ok"], n * UNITS + u)
                    ve.tensor_copy(wbs[:, :, :], rp[:, :, :]).then_inc(s["wb_ok"], 1)
                    dve.wait_ge(s["wb_ok"], n * UNITS + u + 1)
                    dve.wait_ge(s["l2_ps"], n * UNITS + u + 1)
                    if u % NG != 1:
                        prev = {0: 3 * (u // NG), 2: 3 * (u // NG) + 1, 3: 3 * (u // NG) + 2}[u % NG]
                        dve.wait_ge(s["acc_ok"], START["acc_ok"] + n * NP * 3 + prev)
                    gg = u % NG
                    ve.scalar_tensor_tensor(cw[:, u % 2], rp[:, :, :], b2t[:, gg:gg + 1], wbs[:, :, :],
                                            ALU.add, ALU.mult).then_inc(s["c_ok"], 1)
                dve.wait_ge(s["o_ps"], n + 1)
                dve.wait_ge(s["x_out"], START["x_out"] + n * 16)
                ve.tensor_tensor(z[:, :, :], mtok,
                                 bo_b[:, :].rearrange("p (o c) -> p o c", o=1).to_broadcast([P, B, C]),
                                 ALU.add).then_inc(s["fin"], 1)
                dve.wait_ge(s["fin"], START["fin"] + n + 1)
                layer_stats("st5", z, n)
                q = Steps(dve, s["ap5"], n, 5)
                dve.wait_ge(s["sm5"], n * SMALL + SMALL)
                normalise(q, z, z, tiny[:, RS, :])
                q.settle()
                q.did(ve.tensor_tensor(z[:, :, :], z[:, :, :], xp[:, :, :], ALU.add))
                q.end()

        @block.tensor
        def _(pe):
            te = nc.tensor
            pe.sem_inc(s["cm_ps"], START["cm_ps"])
            pe.wait_ge(s["w_in"], W_ALL)
            pe.wait_ge(s["konst"], KONST)
            pe.wait_ge(s["w_rest"], W_REST)

            def to_channels(src, name):
                for k in range(KB):
                    for j in range(B):
                        t = te.transpose(mp[:, k, j * P:(j + 1) * P], src[:, j, k * P:(k + 1) * P], ident[:, :])
                t.then_inc(s[name], 1)

            def to_tokens(src, name):
                v = dense(src)
                for j in range(B):
                    for k in range(KB):
                        t = te.transpose(mtok[:, j, k * P:(k + 1) * P], v[:, k, j * P:(j + 1) * P], ident[:, :])
                t.then_inc(s[name], 1)

            def project(w, rhs, name, m0=0):
                nk = w.shape[1]
                for m in range(2):
                    for k in range(nk):
                        c = (m0 + m) * P
                        t = te.matmul(mp[:, m, :], w[:, k, c:c + P], rhs[:, k, :], start=k == 0, stop=k == nk - 1)
                t.then_inc(s[name], 1)

            with pe.Fori(0, NCH) as n:
                pe.wait_ge(s["ap0"], n * 8 + 8)
                pe.wait_ge(s["fin"], START["fin"] + n)
                to_channels(nrm, "t1_ps")
                pe.wait_ge(s["a_t"], n * SHIFT + SHIFT)
                pe.wait_ge(s["mix1"], n * MIX1 + 2)
                project(wk, dense(XK), "k_ps")
                pe.wait_ge(s["kvr"], n * 3 + 1)
                pe.wait_ge(s["mix1"], n * MIX1 + 4)
                project(wv, dense(XV), "k_ps")
                pe.wait_ge(s["kvr"], n * 3 + 2)
                pe.wait_ge(s["mix1"], n * MIX1 + 6)
                project(wr, dense(XR), "k_ps")
                pe.wait_ge(s["kvr"], n * 3 + 3)
                pe.wait_ge(s["wkv"], n * WKV + WKV)
                project(wo, dense(Y), "u_ps")
                pe.wait_ge(s["xh1"], n + 1)
                pe.wait_ge(s["lif1"], n * LIF + 3)
                te.transpose(mp[0:1, 0, 0:P], mxl[:, :], ident[:, :]).then_inc(s["f1_ps"], 1)
                pe.wait_ge(s["lif1"], n * LIF + LIF)
                to_tokens(S, "s1_ps")
                pe.wait_ge(s["x1_ok"], n + 1)
                pe.wait_ge(s["ap2"], n * 4 + 4)
                to_channels(nrm, "t2_ps")
                pe.wait_ge(s["c_t"], n * SHIFT + SHIFT)
                pe.wait_ge(s["mix2"], n * MIX2 + 2)
                project(fwr, dense(XR), "r2_ps")
                pe.wait_ge(s["er2"], n + 1)
                pe.wait_ge(s["mix2"], n * MIX2 + 4)
                for r in range(4):
                    if r:
                        pe.wait_ge(s["relu"], n * 4 + r)
                    project(fwk, dense(XK), "fk_ps", 2 * r)
                pe.wait_ge(s["relu"], n * 4 + 4)
                pe.wait_ge(s["sq"], n * 4 + 4)
                project(fwv, kk, "kv_ps")
                pe.wait_ge(s["gate"], n * 3 + 3)
                pe.wait_ge(s["lif2"], n * LIF + 3)
                te.transpose(mp[0:1, 0, 0:P], mxl[:, :], ident[:, :]).then_inc(s["f2_ps"], 1)
                pe.wait_ge(s["lif2"], n * LIF + LIF)
                to_tokens(S, "s2_ps")
                pe.wait_ge(s["x2_ok"], n + 1)
                pe.wait_ge(s["ap4"], n * 4 + 4)
                to_channels(nrm, "t4_ps")
                pe.wait_ge(s["y_ok"], n + 1)
                for q in range(NP):
                    if q:
                        pe.wait_ge(s["t_lo"], n * H + 2 * q)
                    for m in range(2):
                        for k in range(KB):
                            t = te.matmul(mp[:, m, :], wm4[:, k, 2 * q + m].rearrange("p r i -> p (r i)"),
                                          y_t[:, k, :], start=k == 0, stop=k == KB - 1)
                    t.then_inc(s["pj_ps"], 1)
                pe.wait_ge(s["t_lo"], n * H + H)
                for j in range(B):
                    for h in range(H):
                        t = te.matmul(mlog[:, j * H + h, :], ts[:, h, j * P:(j + 1) * P], embs[:, :],
                                      start=True, stop=True)
                t.then_inc(s["lg_ps"], 1)

                def layer1(i):
                    q, e = i // E, i % E
                    at = n * UNITS * EG + i - 1
                    if i >= 2:
                        pe.wait_ge(s["g_ok"], at)
                    for m in range(2):
                        t = te.matmul(hp[i % 2][:, m, :], w1s[:, e, :], ts[:, 2 * q + m, :], start=True, stop=True)
                    t.then_inc(s["l1_ps"], 1)

                for i in range(2):
                    layer1(i)
                pe.wait_ge(s["route"], n * ROUTE + ROUTE)
                for q in range(NP):
                    for j in range(B):
                        v = wb[:, j * H + 2 * q:j * H + 2 * q + 2, :, :].rearrange("p h r e -> p (h r e)")
                        t = te.transpose(mwt[:, q, j * P:(j + 1) * P], v, identb[:, :])
                t.then_inc(s["wt_ps"], 1)
                for i in range(2, EG):
                    layer1(i)
                pe.wait_ge(s["wt_ok"], n + 1)

                def combine(q):
                    pe.wait_ge(s["acc_ok"], START["acc_ok"] + n * NP * 3 + 3 * q + 3)
                    for m in range(2):
                        r = HD * (2 * q % 4 + m)
                        t = te.matmul(mp[r:r + HD, q // 2, :], stack[:, :], acc[:, q % 2, m, :],
                                      start=True, stop=True)
                    t.then_inc(s["cm_ps"], 1)

                for u in range(UNITS):
                    q, gg = u // NG, u % NG
                    if u:
                        pe.wait_ge(s["c_ok"], n * UNITS + u)
                    for m in range(2):
                        t = te.matmul(rp[:, m, :], pick[:, m, gg, :], wt[:, q, :], start=True, stop=True)
                    t.then_inc(s["wb_ps"], 1)
                    if u + 1 < UNITS:
                        layer1(EG * (u + 1))
                        layer1(EG * (u + 1) + 1)
                    pe.wait_ge(s["g_ok"], n * UNITS * EG + EG * (u + 1))
                    pe.wait_ge(s["wb_ok"], n * UNITS + u + 1)
                    for m in range(2):
                        for j in range(EG):
                            i = EG * u + j
                            t = te.matmul(rp[HD * j:HD * j + HD, m, :], w2[:, EG * gg + j, :], g[i % GS][:, m, :],
                                          start=True, stop=True)
                    t.then_inc(s["l2_ps"], 1)
                    if u + 1 < UNITS:
                        layer1(EG * (u + 1) + 2)
                        layer1(EG * (u + 1) + 3)
                    if gg == 1 and q:
                        combine(q - 1)
                combine(NP - 1)
                pe.wait_ge(s["cm_ok"], n * 2 + 2)
                for j in range(B):
                    for k in range(KB):
                        t = te.matmul(mtok[:, j, :], comb[:, k, j * P:(j + 1) * P], fo[:, k, :],
                                      start=k == 0, stop=k == KB - 1)
                t.then_inc(s["o_ps"], 1)


_INS = ["L0_attn_" + n for n in ("x ln1_s ln1_b ln2_s ln2_b tmk tmv tmr w_decay u_first Wk Wv Wr Wo f_tmk f_tmr "
                                 "fWk fWr fWv").split()] + \
       ["L0_ffn_" + n for n in "Wm bm expert_emb W1 b1 W2 b2 Wo bo".split()]


def kernel(**inputs):
    import numpy as _np
    import concourse.bacc as _bacc
    from concourse.bass_utils import run_bass_kernel_spmd as _run

    nc = _bacc.Bacc("TRN2", target_bir_lowering=False, num_devices=1)
    arrays, args = {}, {}
    for name in _INS:
        arr = _np.ascontiguousarray(inputs[name])
        arrays[f"in_{name}"] = arr
        args[name] = nc.dram_tensor(f"in_{name}", arr.shape, mybir.dt.from_np(arr.dtype), kind="ExternalInput").ap()
    shape = inputs["L0_attn_x"].shape
    out = nc.dram_tensor("out", shape, F32, kind="ExternalOutput").ap()
    build(nc, args, out)
    r = _run(nc, [arrays], core_ids=[0])
    return r.results[0]["out"]
```

```python
from contextlib import ExitStack

import concourse.bass as bass
from concourse import mybir

F32 = mybir.dt.float32
F32R = mybir.dt.float32r
BF16 = mybir.dt.bfloat16
I32 = mybir.dt.int32
ALU = mybir.AluOpType
ACT = mybir.ActivationFunctionType
AX = mybir.AxisListType

P = 128
EPS = 1e-5
O_START = -1e38
FAR = -3e38
VTH = 1.0

STATS = 9
SMALL0, SMALL = 7, 2
MIX1, MIX2 = 6, 4
WKV = 22
LIF = 8
ROUTE = 20
SHIFT = 4

ATTN = """st0 sm0 ap0 t1 at d1 mxk mxv mxr k ke v ve r re o dd mm ex bv pq nm y u xh li ft fl tk x1 sm2 ap2
t2 ct d2 mx2 r2 rr f0 g0 s0 f1 g1 s1 f2 g2 s2 f3 g3 s3 kv0 kv1 kv2 kv3 gt li2 ft2 fl2 tk2 x2 sm3 ap3 sm4 ap4
t4 yt""".split()
HEADS = "pj th tl lg ra rb rc rd re_ l0 wt l1 xc".split()
EXPERTS = HEADS + [f"u{u}{c}" for u in range(16) for c in "abcd"] + "cb1 out n5 e5".split()
EXPERTS.insert(EXPERTS.index("u9d") + 1, "cb0")


MERGED = """pj st0 th sm0 ap0 t1 tl at d1 mxk mxv mxr k lg ke ra rb rc v rd re_ ve r re o l0 wt l1 xc u0a u0b
u0c u0d u1a u1b dd u1c u1d u2a mm u2b ex bv u2c u2d pq u3a nm u3b y u3c u3d u xh u4a u4b li u4c ft
u4d fl u5a tk u5b x1 sm2 u5c u5d u6a u6b ap2 u6c u6d t2 u7a u7b ct u7c d2 u7d u8a mx2 u8b u8c u8d
u9a u9b u9c u9d r2 rr cb0 f0 g0 s0 u10a f1 g1 s1 f2 u10b g2 u10c u10d u11a s2 f3 u11b g3 s3 u11c kv0
kv1 kv2 kv3 gt u11d u12a li2 u12b u12c u12d u13a u13b u13c u13d u14a u14b ft2 u14c u14d fl2 u15a tk2
u15b u15c x2 u15d sm3 ap3 sm4 cb1 ap4 out t4 n5 e5 yt""".split()


def run(order, *parts):
    heads = [next(p, None) for p in parts]
    for label in order:
        for i, p in enumerate(parts):
            if heads[i] == label:
                heads[i] = next(p, None)
    assert not any(heads), heads


START = {"fin": 1, "cm_ps": 1, "ap5": 1, "pj_ps": 1, "l1_ps": 1, "cm_ok": 1, "acc_ok": 1, "x_out": 16}


class Steps:

    def __init__(self, eng, sem, n, per, start=0):
        self.eng, self.sem, self.base, self.per, self.k = eng, sem, n * per + start, per, 0

    def did(self, ins):
        ins.then_inc(self.sem, 1)
        self.k += 1

    def settle(self):
        self.eng.wait_ge(self.sem, self.base + self.k)

    def end(self):
        assert self.k == self.per, (self.k, self.per)
        self.settle()


def build(nc, a, out, chunks=None):
    x = a["L0_attn_x"]
    B, T, C = x.shape
    KB = C // P
    TC = P
    NCH = chunks or T // TC
    SEG = KB * B
    N = B * TC
    TS = TC + 1
    FB = a["L0_attn_fWk"].shape[1] // P
    H = 8
    E, HD, I = a["L0_ffn_W1"].shape
    NP = H // 2
    NG = 4
    EG = E // NG
    UNITS = NP * NG
    GS = 8
    assert HD * EG == P and I == P and KB == 2 and B == 4 and N == 512

    x_d = x.rearrange("b (n p) c -> n p b c", p=TC)
    out_d = out.rearrange("b (n p) c -> n p b c", p=TC)

    with ExitStack() as ctx:
        def sb(name, shape, dt=F32):
            return ctx.enter_context(nc.sbuf_tensor(name, shape, dt))

        def sem(name):
            return ctx.enter_context(nc.semaphore(name))

        wk, wv, wr, wo, fwr, fo = (sb(n, [P, KB, C]) for n in ("wk", "wv", "wr", "wo", "fwr", "fo"))
        fwk = sb("fwk", [P, KB, FB * P])
        fwv = sb("fwv", [P, FB, C])
        wm = sb("wm", [P, KB, C])
        w1s = sb("w1s", [P, E, I], F32R)
        embs = sb("embs", [P, E], F32R)
        embf = sb("embf", [P, E])
        w2 = sb("w2", [P, E, HD])
        b1t = sb("b1t", [P, E])
        b2t = sb("b2t", [P, NG])
        bmt = sb("bmt", [P, KB])
        bo_b = sb("bo_b", [P, C])
        vecs = sb("vecs", [P, 11, KB])
        LN1S, LN1B, LN2S, LN2B, TMK, TMV, TMR, FTMK, FTMR, WDEC, UFIRST = range(11)
        wneg = sb("wneg", [P, KB])
        ident = sb("ident", [P, P])
        identb = sb("identb", [P, P], BF16)
        stack = sb("stack", [P, HD])
        pick = sb("pick", [P, 2, NG, P], BF16)
        desc = sb("desc", [P, E])
        decay = sb("decay", [P, SEG, TS])
        half = sb("half", [P, SEG, TS])
        nhalf = sb("nhalf", [P, B])

        eps4 = sb("eps4", [P, B])
        tick = sb("tick", [P, 2])

        last_a, last_c, last_o, last_p, last_q, last_v1, last_v2 = (
            sb(n, [P, SEG, 1]) for n in ("last_a", "last_c", "last_o", "last_p", "last_q", "last_v1", "last_v2"))

        xt = sb("xt", [P, B, C])
        res = sb("res", [P, B, C])
        xp = sb("xp", [P, B, C])
        xpf = sb("xpf", [P, B, C])
        z = sb("z", [P, B, C])
        stats_a, stats_f = sb("stats_a", [P, B, 6]), sb("stats_f", [P, B, 6])
        mv_a, mv_f = sb("mv_a", [P, B, 2]), sb("mv_f", [P, B, 2])
        tiny_a, tiny_f = sb("tiny_a", [P, 6, B]), sb("tiny_f", [P, 6, B])
        VE, RS, T0, T1, T2, R1 = range(6)
        rs01 = sb("rs01", [P, B])

        buf = [sb(f"buf{i}", [P, SEG, TS]) for i in range(9)]
        y_t = sb("y_t", [P, KB, N])
        mxl = sb("mxl", [P, 1])
        fm = sb("fm", [1, 1])
        flag = sb("flag", [1, 1], I32)
        vtmp = sb("vtmp", [P, SEG, 1])

        ts = sb("ts", [P, H, N], F32R)
        g = sb("g", [P, GS, 2, N])
        cw = sb("cw", [P, 2, 2, N])
        acc = sb("acc", [P, 2, 2, N])
        comb = sb("comb", [P, KB, N])
        t_hi = cw[:, 0].bitcast(F32R)
        t_lo = cw[:, 1].bitcast(F32R)
        rt = sb("rt", [P, 4, B * H, E])
        wbs = rt[:, 0:2].rearrange("p i g e -> p i (g e)")
        rsm = sb("rsm", [P, 3, B * H])
        wb = sb("wb", [P, B * H, 4, E], BF16)
        wt = sb("wt", [P, NP, N], BF16)

        hp = [ctx.enter_context(nc.psum_tensor(f"hp{i}", [P, 2, N], F32)) for i in range(2)]
        rp = ctx.enter_context(nc.psum_tensor("rp", [P, 2, N], F32))
        mp = ctx.enter_context(nc.psum_tensor("mp", [P, 2, N], F32))
        mseg = mp[:, :, :].rearrange("p k (b t) -> p (k b) t", b=B)
        mtok, otok = (t[:, :, :].rearrange("p k n -> p (k n)").rearrange("p (b c) -> p b c", b=B)
                      for t in (mp, hp[0]))
        mspk = mp[:, :, :].bitcast(BF16).rearrange("p k n -> p (k n)")[:, 0:B * C].rearrange("p (b c) -> p b c", b=B)
        mlog = rp[:, 0, :].rearrange("p (g e) -> p g e", e=E)
        mwt = rp[:, :, :].bitcast(BF16).rearrange("p k n -> p (k n)").rearrange("p (q n) -> p q n", q=NP)

        names = """w_in w_rest konst prep x_in st0 sm0 ap0 t1_ps a_t d1 mix1 k_ps kvr wkv pool_wkv act_wkv
        u_ps xh1 lif1 f1_ps s1_ps x1_ok st2 sm2 ap2 t2_ps c_t d2 mix2 r2_ps er2 fk_ps relu sq kv_ps gate
        lif2 f2_ps s2_ps x2_ok st3 sm3 ap3 st4 sm4 ap4 t4_ps y_ok pj_ps t_hi t_lo ts_ok lg_ps route exps
        wt_ps wt_ok l1_ps g_ok l2_ps wb_ps wb_ok c_ok acc_ok cm_ps cm_ok o_ps fin st5 sm5 ap5 x_out slow xc"""
        s = {n: sem(n) for n in names.split()}
        block = ctx.enter_context(nc.Block())

        def cols(t):
            return t[:, :, 1:TS]

        def before(t):
            return t[:, :, 0:TC]

        def blk(t, k):
            return t[:, k * B:(k + 1) * B, :]

        def vec(i, k):
            return vecs[:, i, k:k + 1]

        AT, D, XK, XV, XR = buf[0], buf[1], buf[2], buf[3], buf[4]
        K, V, ER, AB = buf[5], buf[6], buf[7], buf[8]
        O, A2, B2, BV, DD, PS, QS = buf[0], buf[1], buf[2], buf[3], buf[4], buf[5], buf[0]
        NUM, DEN, TV = buf[1], buf[2], buf[3]
        XH, WL1 = buf[6], buf[7]
        WL2 = buf[0]
        S = sb("spikes", [P, KB, N], BF16)

        def dense(t):
            flat = t[:, :, :].rearrange("p s t -> p (s t)")
            return flat[:, 0:KB * N].rearrange("p (k n) -> p k n", k=KB)

        kk = [dense(buf[i]) for i in (1, 3, 5, 8)]
        nrm = buf[8][:, :, :].rearrange("p s t -> p (s t)")[:, 0:B * C].rearrange("p (b c) -> p b c", b=B)

        def seg(t):
            return dense(t).rearrange("p k (b t) -> p (k b) t", b=B)

        w1raw_all = g[:, 0:2].rearrange("p a h n -> p (a h n)").rearrange("p (e i) -> p e i", e=E)

        def w1raw(q):
            return w1raw_all[q, :, :]

        SPREAD = 16 * 4 * (P // HD)
        W_ALL = 16 * (11 + 8 + 4 * 3 + 5)
        KONST = 10 + E + 7 + 1 + 2 + 4 + 2 * NG * 3
        W_REST = 2 + 4 + KB + 1

        @block.sync
        def _(sp):
            sp.sem_inc(s["x_out"], START["x_out"])
            count = [0]

            def load(dst, src):
                sp.dma_start(dst, src).then_inc(s["w_in"], 16)
                count[0] += 16

            with nc.allow_non_contiguous_dma(reason="small vectors"):
                for i, name in enumerate(("ln1_s", "ln1_b", "ln2_s", "ln2_b", "tmk", "tmv", "tmr", "f_tmk",
                                          "f_tmr", "w_decay", "u_first")):
                    load(vecs[:, i, :], a["L0_attn_" + name].rearrange("(k p) -> p k", p=P))
                for t, name in ((wk, "L0_attn_Wk"), (wv, "L0_attn_Wv"), (wr, "L0_attn_Wr"), (wo, "L0_attn_Wo"),
                                (fwr, "L0_attn_fWr"), (fo, "L0_ffn_Wo"), (fwk, "L0_attn_fWk"),
                                (fwv, "L0_attn_fWv")):
                    load(t[:, :, :], a[name].rearrange("(k p) m -> p k m", p=P))
                for r in range(4):
                    q = slice(HD * r, HD * r + HD)
                    load(w1raw(q), a["L0_ffn_W1"].rearrange("e d i -> d e i"))
                    load(embf[q, :], a["L0_ffn_expert_emb"])
                    load(b2t[q, :], a["L0_ffn_b2"].rearrange("(g j) o -> j o g", j=EG)[r])
                load(wm[:, :, :], a["L0_ffn_Wm"].rearrange("(k p) m -> p k m", p=P))
                load(bmt[:, :], a["L0_ffn_bm"].rearrange("(k p) -> p k", p=P))
                load(w2[:, :, :], a["L0_ffn_W2"].rearrange("e i o -> i e o"))
                load(b1t[:, :], a["L0_ffn_b1"].rearrange("e i -> i e"))
                load(bo_b[:, :], a["L0_ffn_bo"].rearrange("(o c) -> o c", o=1).to_broadcast([P, C]))
            assert count[0] == W_ALL, count[0]

            def fetch(n):
                sp.dma_start(xt[:, :, :], x_d[n]).then_inc(s["x_in"], 16)

            def store(m):
                sp.wait_ge(s["ap5"], START["ap5"] + m * 5 + 5)
                sp.dma_start(out_d[m], z[:, :, :]).then_inc(s["x_out"], 16)

            def refetch(n):
                sp.wait_ge(s["ap3"], n * 5)
                fetch(n)

            def spread(m):
                sp.wait_ge(s["l1_ps"], START["l1_ps"] + m * UNITS * EG)
                for r in range(4):
                    if r % 2 == 0:
                        sp.wait_ge(s["t_lo" if r else "t_hi"], m * KB + KB)
                    for j in range(P // HD):
                        sp.dma_start(ts[HD * r:HD * r + HD, j:H:P // HD, :].bitcast(F32),
                                     cw[HD * j:HD * j + HD, r // 2, :, :]).then_inc(s["ts_ok"], 16)

            fetch(0)
            refetch(1)
            with sp.Fori(1, NCH - 1) as n:
                spread(n - 1)
                refetch(n + 1)
                store(n - 1)
            spread(NCH - 2)
            store(NCH - 2)
            spread(NCH - 1)
            store(NCH - 1)
            sp.wait_ge(s["x_out"], START["x_out"] + NCH * 16)

        @block.gpsimd
        def _(pool):
            pl = nc.gpsimd
            pool.sem_inc(s["acc_ok"], START["acc_ok"])
            k = [0]

            def did(ins):
                ins.then_inc(s["konst"], 1)
                k[0] += 1

            def settle():
                pool.wait_ge(s["konst"], k[0])

            for t in (ident, identb, stack):
                did(pl.memset(t[:, :], 0.0))
            did(pl.memset(pick[:, :, :, :], 0.0))
            did(pl.memset(nhalf[:, :], -0.5))
            did(pl.memset(eps4[:, :], EPS))
            did(pl.memset(tick[:, :], 0.0))
            did(pl.memset(half[:, :, :], 0.5))
            did(pl.memset(decay[:, :, :], 0.0))
            did(pl.memset(wb[:, :, :, :], 0.0))
            for e in range(E):
                did(pl.memset(desc[:, e:e + 1], float(E - e)))
            for t in (last_a, last_c, last_p, last_q, last_v1, last_v2):
                did(pl.memset(t[:, :, :], 0.0))
            did(pl.memset(last_o[:, :, :], O_START))
            settle()
            did(pl.memset(half[:, :, 0:1], 0.0))
            for t in (ident, identb):
                did(pl.affine_select(out=t[:, :], in_=t[:, :], compare_op=ALU.not_equal, fill=1.0, base=0,
                                     pattern=[[-1, P]], channel_multiplier=1))
            for r in range(4):
                settle()
                did(pl.affine_select(out=stack[:, :], in_=stack[:, :], compare_op=ALU.not_equal, fill=1.0,
                                     base=-HD * r, pattern=[[-1, HD]], channel_multiplier=1))
            for hh in range(2):
                for gg in range(NG):
                    for part in range(3):
                        settle()
                        v = pick[:, hh, gg, :].rearrange("p (j o) -> p j o", j=EG)
                        did(pl.affine_select(out=v, in_=v, compare_op=ALU.not_equal, fill=1.0,
                                             base=-(64 * hh + E * part + EG * gg),
                                             pattern=[[-1, EG], [0, HD]], channel_multiplier=1))
            settle()
            assert k[0] == KONST, k[0]

            def roots(name, n, mv, tiny, tail=False):
                q = Steps(pool, s["sm" + name], n, SMALL0 if tail else SMALL)
                pool.wait_ge(s["st" + name], n * STATS + STATS)
                q.did(pl.tensor_tensor(tiny[:, VE, :], mv[:, :, 1], eps4[:, :], ALU.add))
                q.settle()
                q.did(pl.tensor_tensor(tiny[:, RS, :], tiny[:, VE, :], nhalf[:, :], ALU.pow))
                if tail:
                    q.settle()
                    q.did(pl.tensor_tensor(tiny[:, T0, :], mv[:, :, 1], tiny[:, RS, :], ALU.mult))
                    q.settle()
                    q.did(pl.tensor_tensor(tiny[:, T1, :], tiny[:, T0, :], tiny[:, RS, :], ALU.mult))
                    q.settle()
                    q.did(pl.tensor_tensor(tiny[:, T2, :], tiny[:, T1, :], eps4[:, :], ALU.add))
                    q.settle()
                    q.did(pl.tensor_tensor(tiny[:, R1, :], tiny[:, T2, :], nhalf[:, :], ALU.pow))
                    q.settle()
                    q.did(pl.tensor_tensor(rs01[:, :], tiny[:, RS, :], tiny[:, R1, :], ALU.mult))
                q.end()

            def attention(n, first=False):
                yield "sm0"
                roots("0", n, mv_a, tiny_a, tail=True)
                q = Steps(pool, s["pool_wkv"], n, 4)
                yield "dd"
                pool.wait_ge(s["wkv"], n * WKV + 2)
                q.did(pl.tensor_tensor(cols(B2), cols(K), cols(O), ALU.subtract))
                yield "bv"
                pool.wait_ge(s["act_wkv"], n * 5 + 2)
                q.did(pl.tensor_tensor(cols(BV), cols(B2), seg(V), ALU.mult))
                yield "nm"
                pool.wait_ge(s["wkv"], n * WKV + 14)
                pool.wait_ge(s["act_wkv"], n * 5 + 4)
                q.did(pl.tensor_tensor(seg(TV), seg(DD), seg(V), ALU.mult))
                q.did(pl.tensor_tensor(seg(DEN), seg(AB), before(QS), ALU.mult))
                q.end()
                yield "sm2"
                roots("2", n, mv_a, tiny_a)
                for r in range(4):
                    yield f"s{r}"
                    pool.wait_ge(s["relu"], n * 4 + r + 1)
                    pl.tensor_tensor(kk[r], kk[r], kk[r], ALU.mult).then_inc(s["sq"], 1)
                yield "sm3"
                roots("3", n, mv_a, tiny_a)
                yield "sm4"
                roots("4", n, mv_a, tiny_a)

            def experts(m):
                q = Steps(pool, s["acc_ok"], m, NP * 3, START["acc_ok"])
                for p in range(NP):
                    for gg in range(1, NG):
                        u = NG * p + gg
                        yield f"u{u}d"
                        pool.wait_ge(s["c_ok"], m * UNITS + u + 1)
                        if gg == 1:
                            pool.wait_ge(s["cm_ps"], START["cm_ps"] + m * 2 + p // 2)
                        old = cw[:, 0] if gg == 1 else acc[:, p % 2]
                        q.did(pl.tensor_tensor(acc[:, p % 2], old, cw[:, u % 2], ALU.add))
                        q.settle()
                q.end()
                yield "n5"
                roots("5", m, mv_f, tiny_f)

            run(ATTN, attention(0, first=True))
            with pool.Fori(1, NCH) as n:
                run(MERGED, attention(n), experts(n - 1))
            run(EXPERTS, experts(NCH - 1))

        @block.scalar
        def _(act):
            sc = nc.scalar
            act.sem_inc(s["cm_ok"], START["cm_ok"])
            act.wait_ge(s["w_in"], W_ALL)
            act.wait_ge(s["konst"], KONST)
            sc.activation(wneg[:, :], vecs[:, WDEC, :], ACT.Exp).then_inc(s["prep"], 1)
            act.wait_ge(s["prep"], 1)
            sc.mul(wneg[:, :], wneg[:, :], -1.0).then_inc(s["prep"], 1)

            def shifted(name, ps, last, sv, bv, n):
                q = Steps(act, s[name], n, SHIFT)
                act.wait_ge(s[ps], n + 1)
                q.did(sc.copy(AT[:, :, 0:1], last[:, :, :]))
                for k in range(KB):
                    q.did(sc.activation(cols(blk(AT, k)), mseg[:, k * B:(k + 1) * B, :], ACT.Identity,
                                        bias=vec(bv, k), scale=vec(sv, k)))
                q.settle()
                q.did(sc.copy(last[:, :, :], AT[:, :, TC:TS]))
                q.end()

            def attention(n, first=False):
                yield "at"
                shifted("a_t", "t1_ps", last_a, LN1S, LN1B, n)
                q = Steps(act, s["kvr"], n, 3)
                for i, (label, dst) in enumerate((("ke", cols(K)), ("ve", seg(V)), ("re", seg(ER)))):
                    yield label
                    act.wait_ge(s["k_ps"], n * 3 + i + 1)
                    q.did(sc.copy(dst, mseg))
                q.end()
                yield "ex"
                q = Steps(act, s["act_wkv"], n, 5)
                act.wait_ge(s["wkv"], n * WKV + 9)
                q.did(sc.activation(cols(A2), cols(A2), ACT.Exp))
                act.wait_ge(s["pool_wkv"], n * 4 + 1)
                q.did(sc.activation(cols(B2), cols(B2), ACT.Exp))
                q.did(sc.activation(seg(AB), seg(AB), ACT.Exp, scale=-1.0))
                q.did(sc.activation(seg(DD), seg(DD), ACT.Exp))
                q.did(sc.activation(seg(ER), seg(ER), ACT.Exp, scale=-1.0))
                q.end()
                yield "xh"
                act.wait_ge(s["u_ps"], n + 1)
                sc.mul(cols(XH), mseg, 0.5).then_inc(s["xh1"], 1)
                yield "ct"
                shifted("c_t", "t2_ps", last_c, LN2S, LN2B, n)
                yield "rr"
                act.wait_ge(s["r2_ps"], n + 1)
                sc.activation(seg(ER), mseg, ACT.Tanh, scale=0.5).then_inc(s["er2"], 1)
                for r in range(4):
                    yield f"g{r}"
                    act.wait_ge(s["fk_ps"], n * 4 + r + 1)
                    sc.activation(kk[r], mp[:, :, :], ACT.Relu).then_inc(s["relu"], 1)
                yield "yt"
                act.wait_ge(s["t4_ps"], n + 1)
                act.wait_ge(s["pj_ps"], START["pj_ps"] + n)
                sc.copy(y_t[:, :, :], mp[:, :, :]).then_inc(s["y_ok"], 1)

            def experts(m):
                yield "th"
                act.wait_ge(s["pj_ps"], START["pj_ps"] + m + 1)
                for k in range(KB):
                    sc.activation(t_hi[:, k, :], hp[0][:, k, :], ACT.Identity,
                                  bias=bmt[:, k:k + 1]).then_inc(s["t_hi"], 1)
                yield "ra"
                act.wait_ge(s["route"], m * ROUTE + 2)
                sc.activation(rt[:, 1], rt[:, 0], ACT.Exp).then_inc(s["exps"], 1)

                def gelu(i):
                    act.wait_ge(s["l1_ps"], START["l1_ps"] + m * UNITS * EG + i + 1)
                    u = i // EG
                    if u >= 2 and i % EG == 0:
                        act.wait_ge(s["l2_ps"], m * UNITS + u - 1)
                    e = i % E
                    sc.activation(g[:, i % GS], hp[i % 2][:, :, :], ACT.Gelu,
                                  bias=b1t[:, e:e + 1]).then_inc(s["g_ok"], 1)

                yield "l1"
                gelu(0)
                gelu(1)
                yield "xc"
                act.wait_ge(s["ap3"], m * 5 + 5)
                act.wait_ge(s["ap5"], START["ap5"] + m * 5)
                sc.copy(xpf[:, :, :], xp[:, :, :]).then_inc(s["xc"], 1)
                for u in range(UNITS):
                    for c in range(EG):
                        yield f"u{u}{'abcd'[c]}"
                        if EG * u + 2 + c < UNITS * EG:
                            gelu(EG * u + 2 + c)
                    if u == 9 or u == UNITS - 1:
                        c = u // 10
                        yield f"cb{c}"
                        act.wait_ge(s["cm_ps"], START["cm_ps"] + m * 2 + c + 1)
                        sc.copy(comb[:, c, :], rp[:, c, :]).then_inc(s["cm_ok"], 1)

            run(ATTN, attention(0, first=True))
            with act.Fori(1, NCH) as n:
                run(MERGED, attention(n), experts(n - 1))
            run(EXPERTS, experts(NCH - 1))

        @block.vector
        def _(dve):
            ve = nc.vector
            dve.sem_inc(s["fin"], START["fin"])
            dve.sem_inc(s["ap5"], START["ap5"])
            dve.wait_ge(s["w_in"], W_ALL)
            dve.wait_ge(s["konst"], KONST)
            p = Steps(dve, s["w_rest"], 0, W_REST)
            p.did(ve.tensor_copy(w1s[:, :, :], w1raw(slice(0, P))))
            p.did(ve.tensor_copy(embs[:, :], embf[:, :]))
            p.settle()
            for r in (1, 3):
                q = slice(HD * r, HD * r + HD)
                p.did(ve.tensor_tensor(w1s[q, :, :], w1raw(q), w1s[q, :, :].bitcast(F32), ALU.subtract))
                p.did(ve.tensor_tensor(embs[q, :], embf[q, :], embs[q, :].bitcast(F32), ALU.subtract))
            dve.wait_ge(s["prep"], 2)
            for k in range(KB):
                p.did(ve.tensor_scalar(blk(decay, k), blk(decay, k), wneg[:, k:k + 1], None, ALU.add))
            p.settle()
            p.did(ve.memset(decay[:, :, 0:1], FAR))
            p.end()

            def held(q):
                q.did(ve.tensor_copy(tick[:, 1:2], tick[:, 0:1]))

            def layer_stats(name, src, n, stats, mv):
                q = Steps(dve, s[name], n, STATS)
                for j in range(B):
                    q.did(ve.bn_stats(stats[:, j, :], src[:, j, :]))
                q.settle()
                held(q)
                for j in range(B):
                    q.did(ve.bn_aggr(mv[:, j, :], stats[:, j, :]))
                q.end()

            def normalise(q, dst, src, rs, mv):
                for j in range(B):
                    q.did(ve.tensor_scalar(dst[:, j, :], src[:, j, :], mv[:, j, 0:1], rs[:, j:j + 1],
                                           ALU.subtract, ALU.mult))

            def lif(name, ps, last, n, WL, end):
                q = Steps(dve, s[name], n, LIF)
                yield "li" + end
                dve.wait_ge(s["gate" if end else "xh1"], (2 * n + 2) if end else (n + 1))
                q.did(ve.tensor_copy(XH[:, :, 0:1], last[:, :, :]))
                q.settle()
                flat = lambda t: t[:, :, :].rearrange("p s t -> p (s t)")
                q.did(ve.tensor_tensor_scan(flat(WL), flat(half), flat(XH), 0.0, ALU.mult, ALU.add))
                q.settle()
                q.did(ve.tensor_reduce(mxl[:, :], flat(WL), AX.X, ALU.max))
                yield "fl" + end
                dve.wait_ge(s[ps], n + 1)
                q.did(ve.tensor_reduce(fm[:, :], mp[0:1, 0, 0:P], AX.X, ALU.max))
                q.settle()
                q.did(ve.tensor_scalar(flag[:, :], fm[:, :], VTH, None, ALU.is_ge))
                q.settle()
                held(q)
                fires = dve.value_load(flag[0:1, 0:1], min_val=0, max_val=1)
                with dve.If(fires != 0):
                    q.settle()
                    ve.tensor_copy(tick[:, 1:2], tick[:, 0:1]).then_inc(s["slow"], 1)
                    with dve.Fori(1, TS) as t:
                        dve.wait_ge(s["slow"], 2 * t - 1)
                        ve.scalar_tensor_tensor(vtmp[:, :, :], WL[:, :, bass.ds(t - 1, 1)], VTH,
                                                WL[:, :, bass.ds(t - 1, 1)], ALU.is_lt,
                                                ALU.mult).then_inc(s["slow"], 1)
                        dve.wait_ge(s["slow"], 2 * t)
                        ve.scalar_tensor_tensor(WL[:, :, bass.ds(t, 1)], vtmp[:, :, :], 0.5,
                                                XH[:, :, bass.ds(t, 1)], ALU.mult,
                                                ALU.add).then_inc(s["slow"], 1)
                    dve.wait_ge(s["slow"], 2 * TC + 1)
                    dve.sem_clear(s["slow"])
                q.did(ve.tensor_scalar(S[:, :, :].rearrange("p k (b t) -> p (k b) t", b=B), cols(WL), VTH, None, ALU.is_ge))
                q.did(ve.scalar_tensor_tensor(last[:, :, :], WL[:, :, TC:TS], VTH, WL[:, :, TC:TS],
                                              ALU.is_lt, ALU.mult))
                q.end()

            def attention(n, first=False):
                yield "st0"
                dve.wait_ge(s["x_in"], n * 16 + 16)
                layer_stats("st0", xt, n, stats_a, mv_a)
                yield "ap0"
                if not first:
                    dve.wait_ge(s["t4_ps"], n)
                q = Steps(dve, s["ap0"], n, 8)
                dve.wait_ge(s["sm0"], n * SMALL0 + SMALL0)
                normalise(q, res, xt, tiny_a[:, RS, :], mv_a)
                normalise(q, nrm, xt, rs01, mv_a)
                q.end()
                yield "d1"
                dve.wait_ge(s["a_t"], n * SHIFT + 3)
                ve.tensor_tensor(seg(D), cols(AT), before(AT), ALU.subtract).then_inc(s["d1"], 1)
                q = Steps(dve, s["mix1"], n, MIX1)
                for label, dst, m in (("mxk", XK, TMK), ("mxv", XV, TMV), ("mxr", XR, TMR)):
                    yield label
                    if dst is XK:
                        dve.wait_ge(s["d1"], n + 1)
                    for k in range(KB):
                        q.did(ve.scalar_tensor_tensor(blk(seg(dst), k), blk(seg(D), k), vec(m, k),
                                                      before(blk(AT, k)), ALU.mult, ALU.add))
                q.end()
                q = Steps(dve, s["wkv"], n, WKV)
                flat = lambda t: t[:, :, :].rearrange("p s t -> p (s t)")
                yield "o"
                dve.wait_ge(s["kvr"], n * 3 + 3)
                q.did(ve.tensor_copy(K[:, :, 0:1], last_o[:, :, :]))
                q.settle()
                q.did(ve.tensor_tensor_scan(flat(O), flat(decay), flat(K), 0.0, ALU.add, ALU.max))
                q.settle()
                yield "dd"
                for k in range(KB):
                    q.did(ve.scalar_tensor_tensor(cols(blk(A2, k)), before(blk(O, k)), wneg[:, k:k + 1],
                                                  cols(blk(O, k)), ALU.add, ALU.subtract))
                for k in range(KB):
                    q.did(ve.scalar_tensor_tensor(blk(seg(DD), k), cols(blk(K, k)), vec(UFIRST, k),
                                                  before(blk(O, k)), ALU.add, ALU.subtract))
                q.did(ve.tensor_copy(last_o[:, :, :], O[:, :, TC:TS]))
                q.settle()
                yield "mm"
                q.did(ve.tensor_scalar(seg(AB), seg(DD), 0.0, None, ALU.max))
                q.settle()
                q.did(ve.tensor_scalar(seg(DD), seg(DD), 0.0, None, ALU.min))
                yield "pq"
                q.did(ve.memset(A2[:, :, 0:1], 0.0))
                q.did(ve.tensor_copy(BV[:, :, 0:1], last_p[:, :, :]))
                dve.wait_ge(s["pool_wkv"], n * 4 + 2)
                q.did(ve.tensor_copy(B2[:, :, 0:1], last_q[:, :, :]))
                dve.wait_ge(s["act_wkv"], n * 5 + 5)
                q.settle()
                q.did(ve.tensor_tensor_scan(flat(PS), flat(A2), flat(BV), 0.0, ALU.mult, ALU.add))
                q.did(ve.tensor_tensor_scan(flat(QS), flat(A2), flat(B2), 0.0, ALU.mult, ALU.add))
                q.settle()
                q.did(ve.tensor_copy(last_p[:, :, :], PS[:, :, TC:TS]))
                q.did(ve.tensor_copy(last_q[:, :, :], QS[:, :, TC:TS]))
                yield "nm"
                q.did(ve.tensor_tensor(seg(NUM), seg(AB), before(PS), ALU.mult))
                q.settle()
                yield "y"
                dve.wait_ge(s["pool_wkv"], n * 4 + 4)
                q.did(ve.tensor_tensor(seg(NUM), seg(NUM), seg(TV), ALU.add))
                q.did(ve.tensor_tensor(seg(DEN), seg(DEN), seg(DD), ALU.add))
                q.settle()
                q.did(ve.scalar_tensor_tensor(seg(DEN), seg(ER), 1.0, seg(DEN), ALU.add, ALU.mult))
                q.settle()
                q.did(ve.reciprocal(seg(DEN), seg(DEN)))
                q.settle()
                q.did(ve.tensor_tensor(seg(NUM), seg(NUM), seg(DEN), ALU.mult))
                q.end()
                yield from lif("lif1", "f1_ps", last_v1, n, WL1, "")
                yield "x1"
                dve.wait_ge(s["s1_ps"], n + 1)
                ve.tensor_tensor(res[:, :, :], res[:, :, :], mspk, ALU.add).then_inc(s["x1_ok"], 1)
                dve.wait_ge(s["x1_ok"], n + 1)
                layer_stats("st2", res, n, stats_a, mv_a)
                yield "ap2"
                q = Steps(dve, s["ap2"], n, 4)
                dve.wait_ge(s["sm2"], n * SMALL + SMALL)
                normalise(q, nrm, res, tiny_a[:, RS, :], mv_a)
                q.end()
                q = Steps(dve, s["mix2"], n, MIX2)
                yield "d2"
                dve.wait_ge(s["c_t"], n * SHIFT + 3)
                ve.tensor_tensor(seg(D), cols(AT), before(AT), ALU.subtract).then_inc(s["d2"], 1)
                yield "mx2"
                dve.wait_ge(s["d2"], n + 1)
                for dst, m in ((XR, FTMR), (XK, FTMK)):
                    for k in range(KB):
                        q.did(ve.scalar_tensor_tensor(blk(seg(dst), k), blk(seg(D), k), vec(m, k),
                                                      before(blk(AT, k)), ALU.mult, ALU.add))
                q.end()
                q = Steps(dve, s["gate"], n, 2)
                yield "gt"
                dve.wait_ge(s["er2"], n + 1)
                q.did(ve.tensor_scalar(seg(ER), seg(ER), 0.25, 0.25, ALU.mult, ALU.add))
                q.settle()
                dve.wait_ge(s["kv_ps"], n + 1)
                q.did(ve.tensor_tensor(cols(XH), mseg, seg(ER), ALU.mult))
                q.end()
                yield from lif("lif2", "f2_ps", last_v2, n, WL2, "2")
                yield "x2"
                dve.wait_ge(s["s2_ps"], n + 1)
                ve.tensor_tensor(res[:, :, :], res[:, :, :], mspk, ALU.add).then_inc(s["x2_ok"], 1)
                dve.wait_ge(s["x2_ok"], n + 1)
                layer_stats("st3", res, n, stats_a, mv_a)
                yield "ap3"
                q = Steps(dve, s["ap3"], n, 5)
                dve.wait_ge(s["sm3"], n * SMALL + SMALL)
                normalise(q, nrm, res, tiny_a[:, RS, :], mv_a)
                q.settle()
                if not first:
                    dve.wait_ge(s["xc"], n)
                q.did(ve.tensor_tensor(xp[:, :, :], nrm[:, :, :], xt[:, :, :], ALU.add))
                q.end()
                layer_stats("st4", xp, n, stats_a, mv_a)
                yield "ap4"
                q = Steps(dve, s["ap4"], n, 4)
                dve.wait_ge(s["sm4"], n * SMALL + SMALL)
                normalise(q, nrm, xp, tiny_a[:, RS, :], mv_a)
                q.end()

            def experts(m):
                yield "tl"
                dve.wait_ge(s["t_hi"], m * KB + KB)
                for k in range(KB):
                    ve.scalar_tensor_tensor(t_lo[:, k, :], hp[0][:, k, :], bmt[:, k:k + 1],
                                            cw[:, 0, k, :], ALU.add, ALU.subtract).then_inc(s["t_lo"], 1)
                q = Steps(dve, s["route"], m, ROUTE)
                d, ex, hot, tmp = (rt[:, i] for i in range(4))
                mx = rsm[:, 0, :]

                def wide(v):
                    return v.rearrange("p (g o) -> p g o", o=1).to_broadcast([P, B * H, E])

                first = desc[:, :].rearrange("p (o e) -> p o e", o=1).to_broadcast([P, B * H, E])
                yield "lg"
                dve.wait_ge(s["lg_ps"], m + 1)
                q.did(ve.tensor_reduce(mx, mlog, AX.X, ALU.max))
                q.settle()
                q.did(ve.tensor_tensor(d, mlog, wide(mx), ALU.subtract))
                q.settle()
                yield "rb"
                q.did(ve.scalar_tensor_tensor(tmp, d, 0.0, first, ALU.is_equal, ALU.mult))
                q.settle()
                q.did(ve.tensor_reduce(mx, tmp, AX.X, ALU.max))
                q.settle()
                q.did(ve.tensor_tensor(hot, tmp, wide(mx), ALU.is_equal))
                q.settle()
                dve.wait_ge(s["exps"], m + 1)
                q.did(ve.scalar_tensor_tensor(d, hot, FAR, d, ALU.mult, ALU.add))
                q.settle()
                yield "rc"
                q.did(ve.tensor_reduce(mx, d, AX.X, ALU.max))
                q.settle()
                q.did(ve.tensor_tensor(d, d, wide(mx), ALU.subtract))
                q.settle()
                q.did(ve.scalar_tensor_tensor(tmp, d, 0.0, first, ALU.is_equal, ALU.mult))
                q.settle()
                q.did(ve.tensor_reduce(mx, tmp, AX.X, ALU.max))
                q.settle()
                q.did(ve.tensor_tensor(tmp, tmp, wide(mx), ALU.is_equal))
                q.settle()
                yield "rd"
                q.did(ve.tensor_tensor(hot, hot, tmp, ALU.add))
                q.did(ve.tensor_reduce(rsm[:, 1, :], ex, AX.X, ALU.add))
                q.settle()
                q.did(ve.reciprocal(rsm[:, 2, :], rsm[:, 1, :]))
                q.did(ve.tensor_tensor(hot, hot, ex, ALU.mult))
                q.settle()
                q.did(ve.tensor_tensor(hot, hot, wide(rsm[:, 2, :]), ALU.mult))
                q.settle()
                yield "re_"
                q.did(ve.tensor_copy(wb[:, :, 0, :], hot))
                q.settle()
                q.did(ve.tensor_tensor(tmp, hot, wb[:, :, 0, :], ALU.subtract))
                q.settle()
                q.did(ve.tensor_copy(wb[:, :, 1, :], tmp))
                q.settle()
                q.did(ve.tensor_tensor(wb[:, :, 2, :], tmp, wb[:, :, 1, :], ALU.subtract))
                q.end()
                yield "wt"
                dve.wait_ge(s["wt_ps"], m + 1)
                ve.tensor_copy(wt[:, :, :], mwt).then_inc(s["wt_ok"], 1)
                for u in range(UNITS):
                    yield f"u{u}a"
                    dve.wait_ge(s["wb_ps"], m * UNITS + u + 1)
                    if u:
                        dve.wait_ge(s["c_ok"], m * UNITS + u)
                    ve.tensor_copy(wbs[:, :, :], rp[:, :, :]).then_inc(s["wb_ok"], 1)
                    dve.wait_ge(s["wb_ok"], m * UNITS + u + 1)
                    yield f"u{u}c"
                    dve.wait_ge(s["l2_ps"], m * UNITS + u + 1)
                    if u % NG != 1:
                        prev = {0: 3 * (u // NG), 2: 3 * (u // NG) + 1, 3: 3 * (u // NG) + 2}[u % NG]
                        dve.wait_ge(s["acc_ok"], START["acc_ok"] + m * NP * 3 + prev)
                    if u < 2:
                        dve.wait_ge(s["ts_ok"], (m + 1) * SPREAD)
                    gg = u % NG
                    ve.scalar_tensor_tensor(cw[:, u % 2], rp[:, :, :], b2t[:, gg:gg + 1], wbs[:, :, :],
                                            ALU.add, ALU.mult).then_inc(s["c_ok"], 1)
                yield "out"
                dve.wait_ge(s["o_ps"], m + 1)
                dve.wait_ge(s["x_out"], START["x_out"] + m * 16)
                ve.tensor_tensor(z[:, :, :], otok,
                                 bo_b[:, :].rearrange("p (o c) -> p o c", o=1).to_broadcast([P, B, C]),
                                 ALU.add).then_inc(s["fin"], 1)
                dve.wait_ge(s["fin"], START["fin"] + m + 1)
                layer_stats("st5", z, m, stats_f, mv_f)
                yield "e5"
                q = Steps(dve, s["ap5"], m, 5, START["ap5"])
                dve.wait_ge(s["sm5"], m * SMALL + SMALL)
                normalise(q, z, z, tiny_f[:, RS, :], mv_f)
                q.settle()
                dve.wait_ge(s["xc"], m + 1)
                q.did(ve.tensor_tensor(z[:, :, :], z[:, :, :], xpf[:, :, :], ALU.add))
                q.end()

            run(ATTN, attention(0, first=True))
            with dve.Fori(1, NCH) as n:
                run(MERGED, attention(n), experts(n - 1))
            run(EXPERTS, experts(NCH - 1))

        @block.tensor
        def _(pe):
            te = nc.tensor
            pe.sem_inc(s["cm_ps"], START["cm_ps"])
            pe.sem_inc(s["pj_ps"], START["pj_ps"])
            pe.sem_inc(s["l1_ps"], START["l1_ps"])
            pe.wait_ge(s["w_in"], W_ALL)
            pe.wait_ge(s["konst"], KONST)
            pe.wait_ge(s["w_rest"], W_REST)

            def to_channels(src, name):
                for k in range(KB):
                    for j in range(B):
                        t = te.transpose(mp[:, k, j * P:(j + 1) * P], src[:, j, k * P:(k + 1) * P], ident[:, :])
                t.then_inc(s[name], 1)

            def spikes_to_tokens(name):
                for j in range(B):
                    for k in range(KB):
                        t = te.transpose(mspk[:, j, k * P:(k + 1) * P], S[:, k, j * P:(j + 1) * P], identb[:, :])
                t.then_inc(s[name], 1)

            def project(w, rhs, name, m0=0):
                nk = w.shape[1]
                for m in range(2):
                    for k in range(nk):
                        c = (m0 + m) * P
                        t = te.matmul(mp[:, m, :], w[:, k, c:c + P], rhs[:, k, :], start=k == 0, stop=k == nk - 1)
                t.then_inc(s[name], 1)

            def attention(n, first=False):
                yield "t1"
                pe.wait_ge(s["ap0"], n * 8 + 8)
                if not first:
                    pe.wait_ge(s["y_ok"], n)
                to_channels(nrm, "t1_ps")
                for i, (label, w, src) in enumerate((("k", wk, XK), ("v", wv, XV), ("r", wr, XR))):
                    yield label
                    if i == 0:
                        pe.wait_ge(s["a_t"], n * SHIFT + SHIFT)
                    else:
                        pe.wait_ge(s["kvr"], n * 3 + i)
                    pe.wait_ge(s["mix1"], n * MIX1 + 2 * i + 2)
                    project(w, dense(src), "k_ps")
                yield "u"
                pe.wait_ge(s["kvr"], n * 3 + 3)
                pe.wait_ge(s["wkv"], n * WKV + WKV)
                project(wo, dense(NUM), "u_ps")
                yield "ft"
                pe.wait_ge(s["xh1"], n + 1)
                pe.wait_ge(s["lif1"], n * LIF + 3)
                te.transpose(mp[0:1, 0, 0:P], mxl[:, :], ident[:, :]).then_inc(s["f1_ps"], 1)
                yield "tk"
                pe.wait_ge(s["lif1"], n * LIF + LIF)
                spikes_to_tokens("s1_ps")
                yield "t2"
                pe.wait_ge(s["x1_ok"], n + 1)
                pe.wait_ge(s["ap2"], n * 4 + 4)
                to_channels(nrm, "t2_ps")
                yield "r2"
                pe.wait_ge(s["c_t"], n * SHIFT + SHIFT)
                pe.wait_ge(s["mix2"], n * MIX2 + 2)
                project(fwr, dense(XR), "r2_ps")
                for r in range(4):
                    yield f"f{r}"
                    if r:
                        pe.wait_ge(s["relu"], n * 4 + r)
                    else:
                        pe.wait_ge(s["er2"], n + 1)
                        pe.wait_ge(s["mix2"], n * MIX2 + 4)
                    project(fwk, dense(XK), "fk_ps", 2 * r)
                for r in range(4):
                    yield f"kv{r}"
                    if r == 0:
                        pe.wait_ge(s["relu"], n * 4 + 4)
                    pe.wait_ge(s["sq"], n * 4 + r + 1)
                    for m in range(2):
                        for k in range(2 * r, 2 * r + 2):
                            t = te.matmul(mp[:, m, :], fwv[:, k, m * P:m * P + P], kk[r][:, k % 2, :],
                                          start=k == 0, stop=k == FB - 1)
                    if r == 3:
                        t.then_inc(s["kv_ps"], 1)
                yield "ft2"
                pe.wait_ge(s["gate"], n * 2 + 2)
                pe.wait_ge(s["lif2"], n * LIF + 3)
                te.transpose(mp[0:1, 0, 0:P], mxl[:, :], ident[:, :]).then_inc(s["f2_ps"], 1)
                yield "tk2"
                pe.wait_ge(s["lif2"], n * LIF + LIF)
                spikes_to_tokens("s2_ps")
                yield "t4"
                pe.wait_ge(s["x2_ok"], n + 1)
                pe.wait_ge(s["ap4"], n * 4 + 4)
                to_channels(nrm, "t4_ps")

            def experts(m):
                yield "pj"
                pe.wait_ge(s["y_ok"], m + 1)
                pe.wait_ge(s["fin"], START["fin"] + m)
                for i in range(KB):
                    for k in range(KB):
                        t = te.matmul(hp[0][:, i, :], wm[:, k, i * P:(i + 1) * P], y_t[:, k, :],
                                      start=k == 0, stop=k == KB - 1)
                t.then_inc(s["pj_ps"], 1)
                yield "lg"
                pe.wait_ge(s["ts_ok"], (m + 1) * SPREAD)
                pe.wait_ge(s["cm_ok"], START["cm_ok"] + m * 2)
                for j in range(B):
                    for h in range(H):
                        t = te.matmul(mlog[:, j * H + h, :], ts[:, h, j * P:(j + 1) * P], embs[:, :],
                                      start=True, stop=True)
                t.then_inc(s["lg_ps"], 1)

                def layer1(i):
                    q, e = i // E, i % E
                    if i >= 2:
                        pe.wait_ge(s["g_ok"], m * UNITS * EG + i - 1)
                    for k in range(2):
                        t = te.matmul(hp[i % 2][:, k, :], w1s[:, e, :], ts[:, 2 * q + k, :], start=True, stop=True)
                    t.then_inc(s["l1_ps"], 1)

                yield "l0"
                layer1(0)
                layer1(1)
                yield "wt"
                pe.wait_ge(s["route"], m * ROUTE + ROUTE)
                for q in range(NP):
                    for j in range(B):
                        v = wb[:, j * H + 2 * q:j * H + 2 * q + 2, :, :].rearrange("p h r e -> p (h r e)")
                        t = te.transpose(mwt[:, q, j * P:(j + 1) * P], v, identb[:, :])
                t.then_inc(s["wt_ps"], 1)
                yield "l1"
                layer1(2)
                layer1(3)

                def combine(c):
                    pe.wait_ge(s["acc_ok"], START["acc_ok"] + m * NP * 3 + 6 * c + 6)
                    for i in range(4):
                        t = te.matmul(rp[HD * i:HD * i + HD, c, :], stack[:, :], acc[:, i // 2, i % 2, :],
                                      start=True, stop=True)
                    t.then_inc(s["cm_ps"], 1)

                for u in range(UNITS):
                    q, gg = u // NG, u % NG
                    yield f"u{u}a"
                    if u == 0:
                        pe.wait_ge(s["wt_ok"], m + 1)
                    else:
                        pe.wait_ge(s["c_ok"], m * UNITS + u)
                    if u == 10:
                        pe.wait_ge(s["cm_ok"], START["cm_ok"] + m * 2 + 1)
                    for i in range(2):
                        t = te.matmul(rp[:, i, :], pick[:, i, gg, :], wt[:, q, :], start=True, stop=True)
                    t.then_inc(s["wb_ps"], 1)
                    if u + 1 < UNITS:
                        layer1(EG * (u + 1))
                        yield f"u{u}b"
                        layer1(EG * (u + 1) + 1)
                    yield f"u{u}c"
                    pe.wait_ge(s["g_ok"], m * UNITS * EG + EG * (u + 1))
                    pe.wait_ge(s["wb_ok"], m * UNITS + u + 1)
                    for i in range(2):
                        for j in range(EG):
                            t = te.matmul(rp[HD * j:HD * j + HD, i, :], w2[:, EG * gg + j, :],
                                          g[:, (EG * u + j) % GS, i, :], start=True, stop=True)
                    t.then_inc(s["l2_ps"], 1)
                    if u + 1 < UNITS:
                        yield f"u{u}d"
                        layer1(EG * (u + 1) + 2)
                        layer1(EG * (u + 1) + 3)
                    if u == 9:
                        yield "cb0"
                        pe.wait_ge(s["c_ok"], m * UNITS + u + 1)
                        combine(0)
                yield "cb1"
                pe.wait_ge(s["c_ok"], m * UNITS + UNITS)
                combine(1)
                yield "out"
                pe.wait_ge(s["cm_ok"], START["cm_ok"] + m * 2 + 2)
                for j in range(B):
                    for k in range(KB):
                        t = te.matmul(otok[:, j, :], comb[:, k, j * P:(j + 1) * P], fo[:, k, :],
                                      start=k == 0, stop=k == KB - 1)
                t.then_inc(s["o_ps"], 1)

            run(ATTN, attention(0, first=True))
            with pe.Fori(1, NCH) as n:
                run(MERGED, attention(n), experts(n - 1))
            run(EXPERTS, experts(NCH - 1))


_INS = ["L0_attn_" + n for n in ("x ln1_s ln1_b ln2_s ln2_b tmk tmv tmr w_decay u_first Wk Wv Wr Wo f_tmk f_tmr "
                                 "fWk fWr fWv").split()] + \
       ["L0_ffn_" + n for n in "Wm bm expert_emb W1 b1 W2 b2 Wo bo".split()]


def kernel(**inputs):
    import numpy as _np
    import concourse.bacc as _bacc
    from concourse.bass_utils import run_bass_kernel_spmd as _run

    nc = _bacc.Bacc("TRN2", target_bir_lowering=False, num_devices=1)
    arrays, args = {}, {}
    for name in _INS:
        arr = _np.ascontiguousarray(inputs[name])
        arrays[f"in_{name}"] = arr
        args[name] = nc.dram_tensor(f"in_{name}", arr.shape, mybir.dt.from_np(arr.dtype), kind="ExternalInput").ap()
    shape = inputs["L0_attn_x"].shape
    out = nc.dram_tensor("out", shape, F32, kind="ExternalOutput").ap()
    build(nc, args, out)
    r = _run(nc, [arrays], core_ids=[0])
    return r.results[0]["out"]
```

```python
from contextlib import ExitStack

import concourse.bass as bass
from concourse import mybir

F32 = mybir.dt.float32
F32R = mybir.dt.float32r
BF16 = mybir.dt.bfloat16
I32 = mybir.dt.int32
ALU = mybir.AluOpType
ACT = mybir.ActivationFunctionType
AX = mybir.AxisListType

P = 128
EPS = 1e-5
O_START = -1e38
FAR = -3e38
VTH = 1.0

STATS = 9
SMALL0, SMALL = 7, 2
MIX1, MIX2 = 6, 4
WKV = 22
LIF = 8
ROUTE = 20
SHIFT = 4

MIX = """xl st0 sm0 ap0 t1 at d1 mxk mxv mxr k k_ ke v v_ ve r r_ re o dd mm ex bv pq nm y u u_ xh li ft fl""".split()
CHANNEL = """tk x1 sm2 ap2 t2 ct d2 mx2 r2 r2_ rr f0 f0_ g0 s0 f1 f1_ g1 s1 f2 f2_ g2 s2 f3 f3_ g3 s3 kv kv1 kv2 kv3 xf gt li2 ft2 fl2 tk2
x2 sm3 ap3 sm4 ap4 t4 yt pj pj_ th tl lg ra rb rc rd re_ sp""".split()
EXPERTS = "l0 wt l1 xc".split() + [f"u{u}{c}" for u in range(16) for c in "abcde"]
TAIL = "cb1 out n5 e5 st".split()
EXPERTS.insert(EXPERTS.index("u9e") + 1, "cb0")


MERGED = """cb1 out n5 e5 l0 wt l1 tk xc u0a x1 xl u0b st0 u0c sm2 ap2 u0d u0e u1a t2 u1b sm0 ap0 u1c ct u1d u1e
st t1 u2a u2b d2 mx2 at u2c r2 u2d r2_ u2e rr f0 u3a f0_ u3b g0 u3c s0 u3d f1 u3e f1_ u4a d1 mxk mxv
u4b g1 u4c s1 u4d mxr k k_ u4e ke v v_ u5a u5b u5c ve u5d r u5e r_ u6a u6b u6c re o dd u6d f2 u6e
f2_ u7a u7b g2 s2 u7c mm u7d f3 f3_ u7e g3 s3 kv u8a u8b ex u8c kv1 u8d kv2 u8e kv3 xf u9a bv pq u9b
gt li2 u9c u9d ft2 fl2 u9e cb0 tk2 u10a x2 u10b u10c sm3 u10d u10e ap3 u11a nm u11b u11c sm4 u11d
u11e u12a ap4 u12b u12c u12d t4 u12e y yt pj pj_ u13a u13b th tl u13c u13d u13e u14a u u_ u14b xh li
u14c u14d lg u14e u15a ra u15b rb u15c u15d u15e rc ft rd re_ sp fl""".split()


def run(order, *parts):
    heads = [next(p, None) for p in parts]
    for label in order:
        for i, p in enumerate(parts):
            if heads[i] == label:
                heads[i] = next(p, None)
    assert not any(heads), heads


START = {"fin": 1, "cm_ps": 1, "ap5": 1, "l1_ps": 1, "cm_ok": 1, "acc_ok": 1, "x_out": 16, "hp_ok": 1}

READ_OUT = {"t1": ("a_t", SHIFT, 3), "k": ("kvr", 3, 1), "v": ("kvr", 3, 2), "r": ("kvr", 3, 3),
            "u": ("xh1", 1, 1), "ft": ("lif1", LIF, 4), "tk": ("x1_ok", 1, 1), "t2": ("c_t", SHIFT, 3),
            "r2": ("er2", 1, 1), "f0": ("relu", 4, 1), "f1": ("relu", 4, 2), "f2": ("relu", 4, 3),
            "f3": ("relu", 4, 4), "kv": ("gate", 2, 2), "ft2": ("lif2", LIF, 4), "tk2": ("x2_ok", 1, 1),
            "t4": ("y_ok", 1, 1), "pj": ("t_lo", 2, 2), "lg": ("route", ROUTE, 2),
            "wt": ("wt_ok", 1, 1)}


class Steps:

    def __init__(self, eng, sem, n, per, start=0):
        self.eng, self.sem, self.base, self.per, self.k = eng, sem, n * per + start, per, 0

    def did(self, ins):
        ins.then_inc(self.sem, 1)
        self.k += 1

    def settle(self):
        self.eng.wait_ge(self.sem, self.base + self.k)

    def end(self):
        assert self.k == self.per, (self.k, self.per)
        self.settle()


def build(nc, a, out, chunks=None):
    x = a["L0_attn_x"]
    B, T, C = x.shape
    KB = C // P
    TC = P
    NCH = chunks or T // TC
    SEG = KB * B
    N = B * TC
    TS = TC + 1
    FB = a["L0_attn_fWk"].shape[1] // P
    H = 8
    E, HD, I = a["L0_ffn_W1"].shape
    NP = H // 2
    NG = 4
    EG = E // NG
    UNITS = NP * NG
    TURNS = EG + 1
    GS = 6
    assert HD * EG == P and I == P and KB == 2 and B == 4 and N == 512

    x_d = x.rearrange("b (n p) c -> n p b c", p=TC)
    out_d = out.rearrange("b (n p) c -> n p b c", p=TC)

    with ExitStack() as ctx:
        def sb(name, shape, dt=F32):
            return ctx.enter_context(nc.sbuf_tensor(name, shape, dt))

        def sem(name):
            return ctx.enter_context(nc.semaphore(name))

        wk, wv, wr, wo, fwr, fo = (sb(n, [P, KB, C]) for n in ("wk", "wv", "wr", "wo", "fwr", "fo"))
        fwk = sb("fwk", [P, KB, FB * P])
        fwv = sb("fwv", [P, FB, C])
        wm = sb("wm", [P, KB, C])
        w1s = sb("w1s", [P, E, I], F32R)
        embs = sb("embs", [P, P // HD, E])
        embf = sb("embf", [P, E])
        w2 = sb("w2", [P, E, HD])
        b1t = sb("b1t", [P, E])
        b2t = sb("b2t", [P, NG])
        bmt = sb("bmt", [P, KB])
        bo_b = sb("bo_b", [P, C])
        vecs = sb("vecs", [P, 11, KB])
        LN1S, LN1B, LN2S, LN2B, TMK, TMV, TMR, FTMK, FTMR, WDEC, UFIRST = range(11)
        wneg = sb("wneg", [P, KB])
        ident = sb("ident", [P, P])
        identb = sb("identb", [P, P], BF16)
        stack = sb("stack", [P, HD])
        pick = sb("pick", [P, 2, NG, P], BF16)
        desc = sb("desc", [P, E])
        decay = sb("decay", [P, SEG, TS])
        half = sb("half", [P, SEG, TS], BF16)
        nhalf = sb("nhalf", [P, B])

        eps4 = sb("eps4", [P, B])
        tick = sb("tick", [P, 2])

        last_a, last_c, last_o, last_p, last_q, last_v1, last_v2 = (
            sb(n, [P, SEG, 1]) for n in ("last_a", "last_c", "last_o", "last_p", "last_q", "last_v1", "last_v2"))

        res = sb("res", [P, B, C])
        res2 = sb("res2", [P, B, C])
        xp = sb("xp", [P, B, C])
        xpf = sb("xpf", [P, B, C])
        stats_a, stats_c, stats_f = (sb(n, [P, B, 6]) for n in ("stats_a", "stats_c", "stats_f"))
        mv_a, mv_c, mv_f = (sb(n, [P, B, 2]) for n in ("mv_a", "mv_c", "mv_f"))
        tiny_a, tiny_c, tiny_f = (sb(n, [P, 6, B]) for n in ("tiny_a", "tiny_c", "tiny_f"))
        VE, RS, T0, T1, T2, R1 = range(6)
        rs01 = sb("rs01", [P, B])

        buf = [sb(f"buf{i}", [P, SEG, TS]) for i in range(9)]
        buf2 = [sb(f"buf2_{i}", [P, SEG, TS]) for i in range(7)]
        mxl1, mxl2 = sb("mxl1", [P, 1]), sb("mxl2", [P, 1])
        fm = sb("fm", [1, 1])
        flag = sb("flag", [1, 1], I32)
        vtmp = sb("vtmp", [P, SEG, 1])

        ts = sb("ts", [P, H, N], F32R)
        g = sb("g", [P, GS, 2, N])
        cw = sb("cw", [P, 2, 2, N])
        acc = sb("acc", [P, 2, 2, N])
        comb = sb("comb", [P, KB, N])
        wbs = sb("wbs", [P, 2, N])
        rsm = sb("rsm", [P, 3, B * H])
        wb = sb("wb", [P, B * H, 4, E], BF16)
        wt = sb("wt", [P, NP, N], BF16)

        hp = [ctx.enter_context(nc.psum_tensor(f"hp{i}", [P, 2, N], F32)) for i in range(2)]
        rp = ctx.enter_context(nc.psum_tensor("rp", [P, 2, N], F32))
        mp = ctx.enter_context(nc.psum_tensor("mp", [P, 2, N], F32))
        mseg = mp[:, :, :].rearrange("p k (b t) -> p (k b) t", b=B)
        mtok, otok = (t[:, :, :].rearrange("p k n -> p (k n)").rearrange("p (b c) -> p b c", b=B)
                      for t in (mp, rp))
        mspk = mp[:, :, :].bitcast(BF16).rearrange("p k n -> p (k n)")[:, 0:B * C].rearrange("p (b c) -> p b c", b=B)
        mlog = mp[:, 0, :].rearrange("p (g e) -> p g e", e=E)
        mwt = mp[:, :, :].bitcast(BF16).rearrange("p k n -> p (k n)").rearrange("p (q n) -> p q n", q=NP)

        names = """w_in w_rest konst prep x_in st0 sm0 ap0 t1_ps a_t d1 mix1 k_ps kvr wkv pool_wkv act_wkv
        u_ps xh1 lif1 f1_ps s1_ps x1_ok st2 sm2 ap2 t2_ps c_t d2 mix2 r2_ps er2 fk_ps relu sq kv_ps gate
        lif2 f2_ps s2_ps x2_ok st3 sm3 ap3 st4 sm4 ap4 t4_ps y_ok xr_in pj_ps t_hi t_lo ts_ok lg_ps route exps
        wt_ps wt_ok l1_ps hp_ok l2_ps wb_ps c_ok acc_ok cm_ps cm_ok o_ps fin st5 sm5 ap5 x_out slow xc"""
        s = {n: sem(n) for n in names.split()}
        block = ctx.enter_context(nc.Block())

        def cols(t):
            return t[:, :, 1:TS]

        def before(t):
            return t[:, :, 0:TC]

        def blk(t, k):
            return t[:, k * B:(k + 1) * B, :]

        def vec(i, k):
            return vecs[:, i, k:k + 1]

        AT, D, XK, XV, XR = buf[0], buf[1], buf[2], buf[3], buf[4]
        K, V, ER, AB = buf[5], buf[6], buf[7], buf[8]
        O, A2, B2, BV, DD, PS, QS = buf[0], buf[1], buf[2], buf[3], buf[4], buf[5], buf[0]
        NUM, DEN, TV = buf[1], buf[2], buf[3]
        XH, WL1 = buf[6], buf[7]
        AT2, D2, XK2, XR2, ER2, XH2, WL2 = (buf2[i] for i in (0, 1, 2, 3, 3, 2, 0))
        S1 = sb("spikes1", [P, KB, N], BF16)

        def dense(t):
            flat = t[:, :, :].rearrange("p s t -> p (s t)")
            return flat[:, 0:KB * N].rearrange("p (k n) -> p k n", k=KB)

        def tokens(t):
            return t[:, :, :].rearrange("p s t -> p (s t)")[:, 0:B * C].rearrange("p (b c) -> p b c", b=B)

        xt = tokens(buf[7])
        nrm = tokens(buf[8])
        kk = [dense(buf2[i]) for i in (1, 5, 4, 6)]
        nrm2 = tokens(buf2[5])
        xr = tokens(buf2[4])
        S2 = dense(buf2[1]).bitcast(BF16).rearrange("p k (h n) -> p (k h) n", h=2)[:, 0:KB, :]
        y_t = dense(buf2[1])
        t_hi, t_lo = (dense(buf2[i]).bitcast(F32R) for i in (4, 6))
        rt = [dense(buf2[i])[:, k, :].rearrange("p (g e) -> p g e", e=E) for i in (2, 3) for k in range(2)]
        z = comb[:, :, :].rearrange("p k n -> p (k n)").rearrange("p (b c) -> p b c", b=B)

        def seg(t):
            return dense(t).rearrange("p k (b t) -> p (k b) t", b=B)

        w1raw_all = g[:, 0:2].rearrange("p a h n -> p (a h n)").rearrange("p (e i) -> p e i", e=E)

        def w1raw(q):
            return w1raw_all[q, :, :]

        SPREAD = 16 * 4 * (P // HD)
        W_ALL = 16 * (11 + 8 + 4 * 3 + 5)
        KONST = 10 + E + 7 + 1 + 2 + 4 + 2 * NG * 3
        W_REST = 2 + 6 + KB + 1

        @block.sync
        def _(sp):
            sp.sem_inc(s["x_out"], START["x_out"])
            count = [0]

            def load(dst, src):
                sp.dma_start(dst, src).then_inc(s["w_in"], 16)
                count[0] += 16

            with nc.allow_non_contiguous_dma(reason="small vectors"):
                for i, name in enumerate(("ln1_s", "ln1_b", "ln2_s", "ln2_b", "tmk", "tmv", "tmr", "f_tmk",
                                          "f_tmr", "w_decay", "u_first")):
                    load(vecs[:, i, :], a["L0_attn_" + name].rearrange("(k p) -> p k", p=P))
                for t, name in ((wk, "L0_attn_Wk"), (wv, "L0_attn_Wv"), (wr, "L0_attn_Wr"), (wo, "L0_attn_Wo"),
                                (fwr, "L0_attn_fWr"), (fo, "L0_ffn_Wo"), (fwk, "L0_attn_fWk"),
                                (fwv, "L0_attn_fWv")):
                    load(t[:, :, :], a[name].rearrange("(k p) m -> p k m", p=P))
                for r in range(4):
                    q = slice(HD * r, HD * r + HD)
                    load(w1raw(q), a["L0_ffn_W1"].rearrange("e d i -> d e i"))
                    load(embf[q, :], a["L0_ffn_expert_emb"])
                    load(b2t[q, :], a["L0_ffn_b2"].rearrange("(g j) o -> j o g", j=EG)[r])
                load(wm[:, :, :], a["L0_ffn_Wm"].rearrange("(k p) m -> p k m", p=P))
                load(bmt[:, :], a["L0_ffn_bm"].rearrange("(k p) -> p k", p=P))
                load(w2[:, :, :], a["L0_ffn_W2"].rearrange("e i o -> i e o"))
                load(b1t[:, :], a["L0_ffn_b1"].rearrange("e i -> i e"))
                load(bo_b[:, :], a["L0_ffn_bo"].rearrange("(o c) -> o c", o=1).to_broadcast([P, C]))
            assert count[0] == W_ALL, count[0]

            def mix(n, first=False):
                yield "xl"
                if not first:
                    sp.wait_ge(s["lif1"], n * LIF)
                sp.dma_start(xt, x_d[n]).then_inc(s["x_in"], 16)

            def channel(m, first=False):
                yield "xf"
                sp.wait_ge(s["kv_ps"], m + 1)
                sp.dma_start(xr, x_d[m]).then_inc(s["xr_in"], 16)
                yield "sp"
                sp.wait_ge(s["l1_ps"], START["l1_ps"] + m * UNITS * EG)
                for r in range(4):
                    if r % 2 == 0:
                        sp.wait_ge(s["t_lo" if r else "t_hi"], m * KB + KB)
                    t = (t_lo if r // 2 else t_hi).bitcast(F32)
                    for j in range(P // HD):
                        sp.dma_start(ts[HD * r:HD * r + HD, j:H:P // HD, :].bitcast(F32),
                                     t[HD * j:HD * j + HD, :, :]).then_inc(s["ts_ok"], 16)

            def experts(m):
                yield from ()

            def tail(m):
                yield "st"
                sp.wait_ge(s["ap5"], START["ap5"] + m * 5 + 5)
                sp.dma_start(out_d[m], z).then_inc(s["x_out"], 16)

            run(MERGED, mix(0, first=True))
            run(MERGED, mix(1), channel(0, first=True))
            run(MERGED, mix(2), channel(1), experts(0))
            with sp.Fori(3, NCH) as n:
                run(MERGED, mix(n), channel(n - 1), experts(n - 2), tail(n - 3))
            run(MERGED, channel(NCH - 1), experts(NCH - 2), tail(NCH - 3))
            run(MERGED, experts(NCH - 1), tail(NCH - 2))
            run(MERGED, tail(NCH - 1))
            sp.wait_ge(s["x_out"], START["x_out"] + NCH * 16)

        @block.gpsimd
        def _(pool):
            pl = nc.gpsimd
            pool.sem_inc(s["acc_ok"], START["acc_ok"])
            k = [0]

            def did(ins):
                ins.then_inc(s["konst"], 1)
                k[0] += 1

            def settle():
                pool.wait_ge(s["konst"], k[0])

            for t in (ident, identb, stack):
                did(pl.memset(t[:, :], 0.0))
            did(pl.memset(pick[:, :, :, :], 0.0))
            did(pl.memset(nhalf[:, :], -0.5))
            did(pl.memset(eps4[:, :], EPS))
            did(pl.memset(tick[:, :], 0.0))
            did(pl.memset(half[:, :, :], 0.5))
            did(pl.memset(decay[:, :, :], 0.0))
            did(pl.memset(wb[:, :, :, :], 0.0))
            for e in range(E):
                did(pl.memset(desc[:, e:e + 1], float(E - e)))
            for t in (last_a, last_c, last_p, last_q, last_v1, last_v2):
                did(pl.memset(t[:, :, :], 0.0))
            did(pl.memset(last_o[:, :, :], O_START))
            settle()
            did(pl.memset(half[:, :, 0:1], 0.0))
            for t in (ident, identb):
                did(pl.affine_select(out=t[:, :], in_=t[:, :], compare_op=ALU.not_equal, fill=1.0, base=0,
                                     pattern=[[-1, P]], channel_multiplier=1))
            for r in range(4):
                settle()
                did(pl.affine_select(out=stack[:, :], in_=stack[:, :], compare_op=ALU.not_equal, fill=1.0,
                                     base=-HD * r, pattern=[[-1, HD]], channel_multiplier=1))
            for hh in range(2):
                for gg in range(NG):
                    for part in range(3):
                        settle()
                        v = pick[:, hh, gg, :].rearrange("p (j o) -> p j o", j=EG)
                        did(pl.affine_select(out=v, in_=v, compare_op=ALU.not_equal, fill=1.0,
                                             base=-(64 * hh + E * part + EG * gg),
                                             pattern=[[-1, EG], [0, HD]], channel_multiplier=1))
            settle()
            assert k[0] == KONST, k[0]

            def roots(name, n, mv, tiny, tail=False):
                q = Steps(pool, s["sm" + name], n, SMALL0 if tail else SMALL)
                pool.wait_ge(s["st" + name], n * STATS + STATS)
                q.did(pl.tensor_tensor(tiny[:, VE, :], mv[:, :, 1], eps4[:, :], ALU.add))
                q.settle()
                q.did(pl.tensor_tensor(tiny[:, RS, :], tiny[:, VE, :], nhalf[:, :], ALU.pow))
                if tail:
                    q.settle()
                    q.did(pl.tensor_tensor(tiny[:, T0, :], mv[:, :, 1], tiny[:, RS, :], ALU.mult))
                    q.settle()
                    q.did(pl.tensor_tensor(tiny[:, T1, :], tiny[:, T0, :], tiny[:, RS, :], ALU.mult))
                    q.settle()
                    q.did(pl.tensor_tensor(tiny[:, T2, :], tiny[:, T1, :], eps4[:, :], ALU.add))
                    q.settle()
                    q.did(pl.tensor_tensor(tiny[:, R1, :], tiny[:, T2, :], nhalf[:, :], ALU.pow))
                    q.settle()
                    q.did(pl.tensor_tensor(rs01[:, :], tiny[:, RS, :], tiny[:, R1, :], ALU.mult))
                q.end()

            def mix(n, first=False):
                yield "sm0"
                roots("0", n, mv_a, tiny_a, tail=True)
                q = Steps(pool, s["pool_wkv"], n, 4)
                yield "dd"
                pool.wait_ge(s["wkv"], n * WKV + 2)
                q.did(pl.tensor_tensor(cols(B2), cols(K), cols(O), ALU.subtract))
                yield "bv"
                pool.wait_ge(s["act_wkv"], n * 5 + 2)
                q.did(pl.tensor_tensor(cols(BV), cols(B2), seg(V), ALU.mult))
                yield "nm"
                pool.wait_ge(s["wkv"], n * WKV + 14)
                pool.wait_ge(s["act_wkv"], n * 5 + 4)
                q.did(pl.tensor_tensor(seg(TV), seg(DD), seg(V), ALU.mult))
                q.did(pl.tensor_tensor(seg(DEN), seg(AB), before(QS), ALU.mult))
                q.end()

            def channel(m, first=False):
                yield "sm2"
                roots("2", m, mv_c, tiny_c)
                for r in range(4):
                    yield f"s{r}"
                    pool.wait_ge(s["relu"], m * 4 + r + 1)
                    pl.tensor_tensor(kk[r], kk[r], kk[r], ALU.mult).then_inc(s["sq"], 1)
                yield "sm3"
                roots("3", m, mv_c, tiny_c)
                yield "sm4"
                roots("4", m, mv_c, tiny_c)

            def experts(m):
                q = Steps(pool, s["acc_ok"], m, NP * 3, START["acc_ok"])
                for p in range(NP):
                    for gg in range(1, NG):
                        u = NG * p + gg
                        yield f"u{u}d"
                        pool.wait_ge(s["c_ok"], m * UNITS + u + 1)
                        if gg == 1:
                            pool.wait_ge(s["cm_ps"], START["cm_ps"] + m * 2 + p // 2)
                        old = cw[:, 0] if gg == 1 else acc[:, p % 2]
                        q.did(pl.tensor_tensor(acc[:, p % 2], old, cw[:, u % 2], ALU.add))
                        q.settle()
                q.end()

            def tail(m):
                yield "n5"
                roots("5", m, mv_f, tiny_f)

            run(MERGED, mix(0, first=True))
            run(MERGED, mix(1), channel(0, first=True))
            run(MERGED, mix(2), channel(1), experts(0))
            with pool.Fori(3, NCH) as n:
                run(MERGED, mix(n), channel(n - 1), experts(n - 2), tail(n - 3))
            run(MERGED, channel(NCH - 1), experts(NCH - 2), tail(NCH - 3))
            run(MERGED, experts(NCH - 1), tail(NCH - 2))
            run(MERGED, tail(NCH - 1))

        @block.scalar
        def _(act):
            sc = nc.scalar
            act.sem_inc(s["cm_ok"], START["cm_ok"])
            act.sem_inc(s["hp_ok"], START["hp_ok"])
            act.wait_ge(s["w_in"], W_ALL)
            act.wait_ge(s["konst"], KONST)
            sc.activation(wneg[:, :], vecs[:, WDEC, :], ACT.Exp).then_inc(s["prep"], 1)
            act.wait_ge(s["prep"], 1)
            sc.mul(wneg[:, :], wneg[:, :], -1.0).then_inc(s["prep"], 1)

            def shifted(name, ps, last, AT, sv, bv, n):
                q = Steps(act, s[name], n, SHIFT)
                act.wait_ge(s[ps], n + 1)
                q.did(sc.copy(AT[:, :, 0:1], last[:, :, :]))
                for k in range(KB):
                    q.did(sc.activation(cols(blk(AT, k)), mseg[:, k * B:(k + 1) * B, :], ACT.Identity,
                                        bias=vec(bv, k), scale=vec(sv, k)))
                q.settle()
                q.did(sc.copy(last[:, :, :], AT[:, :, TC:TS]))
                q.end()

            def mix(n, first=False):
                yield "at"
                shifted("a_t", "t1_ps", last_a, AT, LN1S, LN1B, n)
                q = Steps(act, s["kvr"], n, 3)
                for i, (label, dst) in enumerate((("ke", cols(K)), ("ve", seg(V)), ("re", seg(ER)))):
                    yield label
                    act.wait_ge(s["k_ps"], n * 3 + i + 1)
                    q.did(sc.copy(dst, mseg))
                q.end()
                yield "ex"
                q = Steps(act, s["act_wkv"], n, 5)
                act.wait_ge(s["wkv"], n * WKV + 9)
                q.did(sc.activation(cols(A2), cols(A2), ACT.Exp))
                act.wait_ge(s["pool_wkv"], n * 4 + 1)
                q.did(sc.activation(cols(B2), cols(B2), ACT.Exp))
                q.did(sc.activation(seg(AB), seg(AB), ACT.Exp, scale=-1.0))
                q.did(sc.activation(seg(DD), seg(DD), ACT.Exp))
                q.did(sc.activation(seg(ER), seg(ER), ACT.Exp, scale=-1.0))
                q.end()
                yield "xh"
                act.wait_ge(s["u_ps"], n + 1)
                sc.mul(cols(XH), mseg, 0.5).then_inc(s["xh1"], 1)

            def channel(m, first=False):
                yield "ct"
                shifted("c_t", "t2_ps", last_c, AT2, LN2S, LN2B, m)
                yield "rr"
                act.wait_ge(s["r2_ps"], m + 1)
                sc.activation(seg(ER2), mseg, ACT.Tanh, scale=0.5).then_inc(s["er2"], 1)
                for r in range(4):
                    yield f"g{r}"
                    act.wait_ge(s["fk_ps"], m * 4 + r + 1)
                    if r == 2 and not first:
                        act.wait_ge(s["ts_ok"], m * SPREAD)
                        act.wait_ge(s["lg_ps"], m)
                    sc.activation(kk[r], mp[:, :, :], ACT.Relu).then_inc(s["relu"], 1)
                yield "yt"
                act.wait_ge(s["t4_ps"], m + 1)
                sc.copy(y_t, mp[:, :, :]).then_inc(s["y_ok"], 1)
                yield "th"
                act.wait_ge(s["pj_ps"], m + 1)
                for k in range(KB):
                    sc.activation(t_hi[:, k, :], mp[:, k, :], ACT.Identity,
                                  bias=bmt[:, k:k + 1]).then_inc(s["t_hi"], 1)
                yield "ra"
                act.wait_ge(s["route"], m * ROUTE + 2)
                sc.activation(rt[1], rt[0], ACT.Exp).then_inc(s["exps"], 1)

            def experts(m):
                def take(turn):
                    u, c = turn // TURNS, turn % TURNS
                    if u == UNITS:
                        return
                    if c == EG:
                        act.wait_ge(s["wb_ps"], m * UNITS + u + 1)
                        if u:
                            act.wait_ge(s["c_ok"], m * UNITS + u)
                        sc.copy(wbs[:, :, :], hp[turn % 2][:, :, :]).then_inc(s["hp_ok"], 1)
                        return
                    i = EG * u + c
                    act.wait_ge(s["l1_ps"], START["l1_ps"] + m * UNITS * EG + i + 1)
                    if i >= GS and i % 2 == 0:
                        act.wait_ge(s["l2_ps"], m * UNITS + (i - GS) // EG + 1)
                    e = i % E
                    sc.activation(g[:, i % GS], hp[turn % 2][:, :, :], ACT.Gelu,
                                  bias=b1t[:, e:e + 1]).then_inc(s["hp_ok"], 1)

                yield "l1"
                for turn in range(3):
                    take(turn)
                yield "xc"
                act.wait_ge(s["ap3"], m * 5 + 5)
                act.wait_ge(s["ap5"], START["ap5"] + m * 5)
                sc.copy(xpf[:, :, :], xp[:, :, :]).then_inc(s["xc"], 1)
                for u in range(UNITS):
                    for c in range(TURNS):
                        yield f"u{u}{'abcde'[c]}"
                        take(TURNS * u + 3 + c)
                    if u == 9:
                        yield "cb0"
                        act.wait_ge(s["cm_ps"], START["cm_ps"] + m * 2 + 1)
                        act.wait_ge(s["x_out"], START["x_out"] + m * 16)
                        sc.copy(comb[:, 0, :], rp[:, 0, :]).then_inc(s["cm_ok"], 1)

            def tail(m):
                yield "cb1"
                act.wait_ge(s["cm_ps"], START["cm_ps"] + m * 2 + 2)
                sc.copy(comb[:, 1, :], rp[:, 1, :]).then_inc(s["cm_ok"], 1)

            run(MERGED, mix(0, first=True))
            run(MERGED, mix(1), channel(0, first=True))
            run(MERGED, mix(2), channel(1), experts(0))
            with act.Fori(3, NCH) as n:
                run(MERGED, mix(n), channel(n - 1), experts(n - 2), tail(n - 3))
            run(MERGED, channel(NCH - 1), experts(NCH - 2), tail(NCH - 3))
            run(MERGED, experts(NCH - 1), tail(NCH - 2))
            run(MERGED, tail(NCH - 1))

        @block.vector
        def _(dve):
            ve = nc.vector
            dve.sem_inc(s["fin"], START["fin"])
            dve.sem_inc(s["ap5"], START["ap5"])
            dve.wait_ge(s["w_in"], W_ALL)
            dve.wait_ge(s["konst"], KONST)
            p = Steps(dve, s["w_rest"], 0, W_REST)
            p.did(ve.tensor_copy(w1s[:, :, :], w1raw(slice(0, P))))
            p.did(ve.memset(embs[:, :, :], 0.0))
            p.settle()
            for r in range(4):
                q = slice(HD * r, HD * r + HD)
                p.did(ve.tensor_copy(embs[q, r, :], embf[q, :]))
                if r % 2:
                    p.did(ve.tensor_tensor(w1s[q, :, :], w1raw(q), w1s[q, :, :].bitcast(F32), ALU.subtract))
            dve.wait_ge(s["prep"], 2)
            for k in range(KB):
                p.did(ve.tensor_scalar(blk(decay, k), blk(decay, k), wneg[:, k:k + 1], None, ALU.add))
            p.settle()
            p.did(ve.memset(decay[:, :, 0:1], FAR))
            p.end()

            def held(q):
                q.did(ve.tensor_copy(tick[:, 1:2], tick[:, 0:1]))

            def layer_stats(name, src, n, stats, mv):
                q = Steps(dve, s[name], n, STATS)
                for j in range(B):
                    q.did(ve.bn_stats(stats[:, j, :], src[:, j, :]))
                q.settle()
                held(q)
                for j in range(B):
                    q.did(ve.bn_aggr(mv[:, j, :], stats[:, j, :]))
                q.end()

            def normalise(q, dst, src, rs, mv):
                for j in range(B):
                    q.did(ve.tensor_scalar(dst[:, j, :], src[:, j, :], mv[:, j, 0:1], rs[:, j:j + 1],
                                           ALU.subtract, ALU.mult))

            def lif(name, ps, last, n, XH, WL, mxl, S, end, first):
                q = Steps(dve, s[name], n, LIF)
                yield "li" + end
                dve.wait_ge(s["gate" if end else "xh1"], (2 * n + 2) if end else (n + 1))
                q.did(ve.tensor_copy(XH[:, :, 0:1], last[:, :, :]))
                q.settle()
                flat = lambda t: t[:, :, :].rearrange("p s t -> p (s t)")
                q.did(ve.tensor_tensor_scan(flat(WL), flat(half), flat(XH), 0.0, ALU.mult, ALU.add))
                q.settle()
                q.did(ve.tensor_reduce(mxl[:, :], flat(WL), AX.X, ALU.max))
                yield "fl" + end
                dve.wait_ge(s[ps], n + 1)
                q.did(ve.tensor_reduce(fm[:, :], mp[0:1, 0, 0:P], AX.X, ALU.max))
                q.settle()
                q.did(ve.tensor_scalar(flag[:, :], fm[:, :], VTH, None, ALU.is_ge))
                q.settle()
                held(q)
                fires = dve.value_load(flag[0:1, 0:1], min_val=0, max_val=1)
                with dve.If(fires != 0):
                    q.settle()
                    ve.tensor_copy(tick[:, 1:2], tick[:, 0:1]).then_inc(s["slow"], 1)
                    with dve.Fori(1, TS) as t:
                        dve.wait_ge(s["slow"], 2 * t - 1)
                        ve.scalar_tensor_tensor(vtmp[:, :, :], WL[:, :, bass.ds(t - 1, 1)], VTH,
                                                WL[:, :, bass.ds(t - 1, 1)], ALU.is_lt,
                                                ALU.mult).then_inc(s["slow"], 1)
                        dve.wait_ge(s["slow"], 2 * t)
                        ve.scalar_tensor_tensor(WL[:, :, bass.ds(t, 1)], vtmp[:, :, :], 0.5,
                                                XH[:, :, bass.ds(t, 1)], ALU.mult,
                                                ALU.add).then_inc(s["slow"], 1)
                    dve.wait_ge(s["slow"], 2 * TC + 1)
                    dve.sem_clear(s["slow"])
                if not (end or first):
                    dve.wait_ge(s["s1_ps"], n)
                q.did(ve.tensor_scalar(S[:, :, :].rearrange("p k (b t) -> p (k b) t", b=B), cols(WL), VTH, None, ALU.is_ge))
                q.did(ve.scalar_tensor_tensor(last[:, :, :], WL[:, :, TC:TS], VTH, WL[:, :, TC:TS],
                                              ALU.is_lt, ALU.mult))
                q.end()

            def mix(n, first=False):
                yield "st0"
                dve.wait_ge(s["x_in"], n * 16 + 16)
                layer_stats("st0", xt, n, stats_a, mv_a)
                yield "ap0"
                if not first:
                    dve.wait_ge(s["x1_ok"], n)
                q = Steps(dve, s["ap0"], n, 8)
                dve.wait_ge(s["sm0"], n * SMALL0 + SMALL0)
                normalise(q, res, xt, tiny_a[:, RS, :], mv_a)
                normalise(q, nrm, xt, rs01, mv_a)
                q.end()
                yield "d1"
                dve.wait_ge(s["a_t"], n * SHIFT + 3)
                ve.tensor_tensor(seg(D), cols(AT), before(AT), ALU.subtract).then_inc(s["d1"], 1)
                q = Steps(dve, s["mix1"], n, MIX1)
                for label, dst, m in (("mxk", XK, TMK), ("mxv", XV, TMV), ("mxr", XR, TMR)):
                    yield label
                    if dst is XK:
                        dve.wait_ge(s["d1"], n + 1)
                    for k in range(KB):
                        q.did(ve.scalar_tensor_tensor(blk(seg(dst), k), blk(seg(D), k), vec(m, k),
                                                      before(blk(AT, k)), ALU.mult, ALU.add))
                q.end()
                q = Steps(dve, s["wkv"], n, WKV)
                flat = lambda t: t[:, :, :].rearrange("p s t -> p (s t)")
                yield "o"
                dve.wait_ge(s["kvr"], n * 3 + 3)
                q.did(ve.tensor_copy(K[:, :, 0:1], last_o[:, :, :]))
                q.settle()
                q.did(ve.tensor_tensor_scan(flat(O), flat(decay), flat(K), 0.0, ALU.add, ALU.max))
                q.settle()
                yield "dd"
                for k in range(KB):
                    q.did(ve.scalar_tensor_tensor(cols(blk(A2, k)), before(blk(O, k)), wneg[:, k:k + 1],
                                                  cols(blk(O, k)), ALU.add, ALU.subtract))
                for k in range(KB):
                    q.did(ve.scalar_tensor_tensor(blk(seg(DD), k), cols(blk(K, k)), vec(UFIRST, k),
                                                  before(blk(O, k)), ALU.add, ALU.subtract))
                q.did(ve.tensor_copy(last_o[:, :, :], O[:, :, TC:TS]))
                q.settle()
                yield "mm"
                q.did(ve.tensor_scalar(seg(AB), seg(DD), 0.0, None, ALU.max))
                q.settle()
                q.did(ve.tensor_scalar(seg(DD), seg(DD), 0.0, None, ALU.min))
                yield "pq"
                q.did(ve.memset(A2[:, :, 0:1], 0.0))
                q.did(ve.tensor_copy(BV[:, :, 0:1], last_p[:, :, :]))
                dve.wait_ge(s["pool_wkv"], n * 4 + 2)
                q.did(ve.tensor_copy(B2[:, :, 0:1], last_q[:, :, :]))
                dve.wait_ge(s["act_wkv"], n * 5 + 5)
                q.settle()
                q.did(ve.tensor_tensor_scan(flat(PS), flat(A2), flat(BV), 0.0, ALU.mult, ALU.add))
                q.did(ve.tensor_tensor_scan(flat(QS), flat(A2), flat(B2), 0.0, ALU.mult, ALU.add))
                q.settle()
                q.did(ve.tensor_copy(last_p[:, :, :], PS[:, :, TC:TS]))
                q.did(ve.tensor_copy(last_q[:, :, :], QS[:, :, TC:TS]))
                yield "nm"
                q.did(ve.tensor_tensor(seg(NUM), seg(AB), before(PS), ALU.mult))
                q.settle()
                yield "y"
                dve.wait_ge(s["pool_wkv"], n * 4 + 4)
                q.did(ve.tensor_tensor(seg(NUM), seg(NUM), seg(TV), ALU.add))
                q.did(ve.tensor_tensor(seg(DEN), seg(DEN), seg(DD), ALU.add))
                q.settle()
                q.did(ve.scalar_tensor_tensor(seg(DEN), seg(ER), 1.0, seg(DEN), ALU.add, ALU.mult))
                q.settle()
                q.did(ve.reciprocal(seg(DEN), seg(DEN)))
                q.settle()
                q.did(ve.tensor_tensor(seg(NUM), seg(NUM), seg(DEN), ALU.mult))
                q.end()
                yield from lif("lif1", "f1_ps", last_v1, n, XH, WL1, mxl1, S1, "", first)
            def channel(m, first=False):
                yield "x1"
                dve.wait_ge(s["s1_ps"], m + 1)
                ve.tensor_tensor(res2[:, :, :], res[:, :, :], mspk, ALU.add).then_inc(s["x1_ok"], 1)
                dve.wait_ge(s["x1_ok"], m + 1)
                layer_stats("st2", res2, m, stats_c, mv_c)
                yield "ap2"
                q = Steps(dve, s["ap2"], m, 4)
                if not first:
                    dve.wait_ge(s["t4_ps"], m)
                dve.wait_ge(s["sm2"], m * SMALL + SMALL)
                normalise(q, nrm2, res2, tiny_c[:, RS, :], mv_c)
                q.end()
                q = Steps(dve, s["mix2"], m, MIX2)
                yield "d2"
                dve.wait_ge(s["c_t"], m * SHIFT + 3)
                ve.tensor_tensor(seg(D2), cols(AT2), before(AT2), ALU.subtract).then_inc(s["d2"], 1)
                yield "mx2"
                dve.wait_ge(s["d2"], m + 1)
                for dst, tm in ((XR2, FTMR), (XK2, FTMK)):
                    for k in range(KB):
                        q.did(ve.scalar_tensor_tensor(blk(seg(dst), k), blk(seg(D2), k), vec(tm, k),
                                                      before(blk(AT2, k)), ALU.mult, ALU.add))
                q.end()
                q = Steps(dve, s["gate"], m, 2)
                yield "gt"
                dve.wait_ge(s["er2"], m + 1)
                q.did(ve.tensor_scalar(seg(ER2), seg(ER2), 0.25, 0.25, ALU.mult, ALU.add))
                q.settle()
                dve.wait_ge(s["kv_ps"], m + 1)
                q.did(ve.tensor_tensor(cols(XH2), mseg, seg(ER2), ALU.mult))
                q.end()
                yield from lif("lif2", "f2_ps", last_v2, m, XH2, WL2, mxl2, S2, "2", first)
                yield "x2"
                dve.wait_ge(s["s2_ps"], m + 1)
                ve.tensor_tensor(res2[:, :, :], res2[:, :, :], mspk, ALU.add).then_inc(s["x2_ok"], 1)
                dve.wait_ge(s["x2_ok"], m + 1)
                layer_stats("st3", res2, m, stats_c, mv_c)
                yield "ap3"
                q = Steps(dve, s["ap3"], m, 5)
                dve.wait_ge(s["sm3"], m * SMALL + SMALL)
                normalise(q, nrm2, res2, tiny_c[:, RS, :], mv_c)
                q.settle()
                dve.wait_ge(s["xr_in"], m * 16 + 16)
                if not first:
                    dve.wait_ge(s["xc"], m)
                q.did(ve.tensor_tensor(xp[:, :, :], nrm2, xr, ALU.add))
                q.end()
                layer_stats("st4", xp, m, stats_c, mv_c)
                yield "ap4"
                q = Steps(dve, s["ap4"], m, 4)
                dve.wait_ge(s["sm4"], m * SMALL + SMALL)
                normalise(q, nrm2, xp, tiny_c[:, RS, :], mv_c)
                q.end()

                yield "tl"
                dve.wait_ge(s["t_hi"], m * KB + KB)
                for k in range(KB):
                    ve.scalar_tensor_tensor(t_lo[:, k, :], mp[:, k, :], bmt[:, k:k + 1],
                                            t_hi[:, k, :].bitcast(F32), ALU.add, ALU.subtract).then_inc(s["t_lo"], 1)
                q = Steps(dve, s["route"], m, ROUTE)
                d, ex, hot, tmp = rt
                mx = rsm[:, 0, :]

                def wide(v):
                    return v.rearrange("p (g o) -> p g o", o=1).to_broadcast([P, B * H, E])

                first = desc[:, :].rearrange("p (o e) -> p o e", o=1).to_broadcast([P, B * H, E])
                yield "lg"
                dve.wait_ge(s["lg_ps"], m + 1)
                q.did(ve.tensor_reduce(mx, mlog, AX.X, ALU.max))
                q.settle()
                q.did(ve.tensor_tensor(d, mlog, wide(mx), ALU.subtract))
                q.settle()
                yield "rb"
                q.did(ve.scalar_tensor_tensor(tmp, d, 0.0, first, ALU.is_equal, ALU.mult))
                q.settle()
                q.did(ve.tensor_reduce(mx, tmp, AX.X, ALU.max))
                q.settle()
                q.did(ve.tensor_tensor(hot, tmp, wide(mx), ALU.is_equal))
                q.settle()
                dve.wait_ge(s["exps"], m + 1)
                q.did(ve.scalar_tensor_tensor(d, hot, FAR, d, ALU.mult, ALU.add))
                q.settle()
                yield "rc"
                q.did(ve.tensor_reduce(mx, d, AX.X, ALU.max))
                q.settle()
                q.did(ve.tensor_tensor(d, d, wide(mx), ALU.subtract))
                q.settle()
                q.did(ve.scalar_tensor_tensor(tmp, d, 0.0, first, ALU.is_equal, ALU.mult))
                q.settle()
                q.did(ve.tensor_reduce(mx, tmp, AX.X, ALU.max))
                q.settle()
                q.did(ve.tensor_tensor(tmp, tmp, wide(mx), ALU.is_equal))
                q.settle()
                yield "rd"
                q.did(ve.tensor_tensor(hot, hot, tmp, ALU.add))
                q.did(ve.tensor_reduce(rsm[:, 1, :], ex, AX.X, ALU.add))
                q.settle()
                q.did(ve.reciprocal(rsm[:, 2, :], rsm[:, 1, :]))
                q.did(ve.tensor_tensor(hot, hot, ex, ALU.mult))
                q.settle()
                q.did(ve.tensor_tensor(hot, hot, wide(rsm[:, 2, :]), ALU.mult))
                q.settle()
                yield "re_"
                if not first:
                    dve.wait_ge(s["wt_ps"], m)
                q.did(ve.tensor_copy(wb[:, :, 0, :], hot))
                q.settle()
                q.did(ve.tensor_tensor(tmp, hot, wb[:, :, 0, :], ALU.subtract))
                q.settle()
                q.did(ve.tensor_copy(wb[:, :, 1, :], tmp))
                q.settle()
                q.did(ve.tensor_tensor(wb[:, :, 2, :], tmp, wb[:, :, 1, :], ALU.subtract))
                q.end()

            def experts(m):
                yield "wt"
                dve.wait_ge(s["wt_ps"], m + 1)
                ve.tensor_copy(wt[:, :, :], mwt).then_inc(s["wt_ok"], 1)
                for u in range(UNITS):
                    yield f"u{u}c"
                    dve.wait_ge(s["l2_ps"], m * UNITS + u + 1)
                    dve.wait_ge(s["hp_ok"], START["hp_ok"] + (m * UNITS + u + 1) * TURNS)
                    if u % NG != 1:
                        prev = {0: 3 * (u // NG), 2: 3 * (u // NG) + 1, 3: 3 * (u // NG) + 2}[u % NG]
                        dve.wait_ge(s["acc_ok"], START["acc_ok"] + m * NP * 3 + prev)
                    gg = u % NG
                    ve.scalar_tensor_tensor(cw[:, u % 2], rp[:, :, :], b2t[:, gg:gg + 1], wbs[:, :, :],
                                            ALU.add, ALU.mult).then_inc(s["c_ok"], 1)

            def tail(m):
                yield "out"
                dve.wait_ge(s["o_ps"], m + 1)
                ve.tensor_tensor(z, otok,
                                 bo_b[:, :].rearrange("p (o c) -> p o c", o=1).to_broadcast([P, B, C]),
                                 ALU.add).then_inc(s["fin"], 1)
                dve.wait_ge(s["fin"], START["fin"] + m + 1)
                layer_stats("st5", z, m, stats_f, mv_f)
                yield "e5"
                q = Steps(dve, s["ap5"], m, 5, START["ap5"])
                dve.wait_ge(s["sm5"], m * SMALL + SMALL)
                normalise(q, z, z, tiny_f[:, RS, :], mv_f)
                q.settle()
                dve.wait_ge(s["xc"], m + 1)
                q.did(ve.tensor_tensor(z, z, xpf[:, :, :], ALU.add))
                q.end()

            run(MERGED, mix(0, first=True))
            run(MERGED, mix(1), channel(0, first=True))
            run(MERGED, mix(2), channel(1), experts(0))
            with dve.Fori(3, NCH) as n:
                run(MERGED, mix(n), channel(n - 1), experts(n - 2), tail(n - 3))
            run(MERGED, channel(NCH - 1), experts(NCH - 2), tail(NCH - 3))
            run(MERGED, experts(NCH - 1), tail(NCH - 2))
            run(MERGED, tail(NCH - 1))

        @block.tensor
        def _(pe):
            te = nc.tensor
            pe.sem_inc(s["cm_ps"], START["cm_ps"])
            pe.sem_inc(s["l1_ps"], START["l1_ps"])
            pe.wait_ge(s["w_in"], W_ALL)
            pe.wait_ge(s["konst"], KONST)
            pe.wait_ge(s["w_rest"], W_REST)

            def to_channels(src, name):
                for k in range(KB):
                    for j in range(B):
                        t = te.transpose(mp[:, k, j * P:(j + 1) * P], src[:, j, k * P:(k + 1) * P], ident[:, :])
                t.then_inc(s[name], 1)

            mp_user = [None]

            def take_mp(label, n):
                if mp_user[0]:
                    sem, per, told = READ_OUT[mp_user[0][0]]
                    pe.wait_ge(s[sem], mp_user[0][1] * per + told)
                mp_user[0] = (label, n)

            def spikes_to_tokens(S, name):
                for j in range(B):
                    for k in range(KB):
                        t = te.transpose(mspk[:, j, k * P:(k + 1) * P], S[:, k, j * P:(j + 1) * P], identb[:, :])
                t.then_inc(s[name], 1)

            def project(w, rhs, name, half, m0=0):
                nk = w.shape[1]
                for m in range(2):
                    if m:
                        yield half
                    for k in range(nk):
                        c = (m0 + m) * P
                        t = te.matmul(mp[:, m, :], w[:, k, c:c + P], rhs[:, k, :], start=k == 0, stop=k == nk - 1)
                t.then_inc(s[name], 1)

            def mix(n, first=False):
                yield "t1"
                take_mp("t1", n)
                pe.wait_ge(s["ap0"], n * 8 + 8)
                to_channels(nrm, "t1_ps")
                for i, (label, w, src) in enumerate((("k", wk, XK), ("v", wv, XV), ("r", wr, XR))):
                    yield label
                    take_mp(label, n)
                    pe.wait_ge(s["mix1"], n * MIX1 + 2 * i + 2)
                    yield from project(w, dense(src), "k_ps", label + "_")
                yield "u"
                take_mp("u", n)
                pe.wait_ge(s["wkv"], n * WKV + WKV)
                yield from project(wo, dense(NUM), "u_ps", "u_")
                yield "ft"
                take_mp("ft", n)
                pe.wait_ge(s["lif1"], n * LIF + 3)
                te.transpose(mp[0:1, 0, 0:P], mxl1[:, :], ident[:, :]).then_inc(s["f1_ps"], 1)

            def channel(m, first=False):
                yield "tk"
                take_mp("tk", m)
                pe.wait_ge(s["lif1"], m * LIF + LIF)
                spikes_to_tokens(S1, "s1_ps")
                yield "t2"
                take_mp("t2", m)
                pe.wait_ge(s["ap2"], m * 4 + 4)
                to_channels(nrm2, "t2_ps")
                yield "r2"
                take_mp("r2", m)
                pe.wait_ge(s["mix2"], m * MIX2 + 2)
                yield from project(fwr, dense(XR2), "r2_ps", "r2_")
                for r in range(4):
                    yield f"f{r}"
                    take_mp(f"f{r}", m)
                    if r == 0:
                        pe.wait_ge(s["mix2"], m * MIX2 + 4)
                    yield from project(fwk, dense(XK2), "fk_ps", f"f{r}_", 2 * r)
                yield "kv"
                take_mp("kv", m)
                for r in range(4):
                    if r:
                        yield f"kv{r}"
                    pe.wait_ge(s["sq"], m * 4 + r + 1)
                    for i in range(2):
                        for k in range(2 * r, 2 * r + 2):
                            t = te.matmul(mp[:, i, :], fwv[:, k, i * P:i * P + P], kk[r][:, k % 2, :],
                                          start=k == 0, stop=k == FB - 1)
                t.then_inc(s["kv_ps"], 1)
                yield "ft2"
                take_mp("ft2", m)
                pe.wait_ge(s["lif2"], m * LIF + 3)
                te.transpose(mp[0:1, 0, 0:P], mxl2[:, :], ident[:, :]).then_inc(s["f2_ps"], 1)
                yield "tk2"
                take_mp("tk2", m)
                pe.wait_ge(s["lif2"], m * LIF + LIF)
                spikes_to_tokens(S2, "s2_ps")
                yield "t4"
                take_mp("t4", m)
                pe.wait_ge(s["ap4"], m * 4 + 4)
                to_channels(nrm2, "t4_ps")
                yield "pj"
                take_mp("pj", m)
                pe.wait_ge(s["y_ok"], m + 1)
                for i in range(KB):
                    if i:
                        yield "pj_"
                    for k in range(KB):
                        t = te.matmul(mp[:, i, :], wm[:, k, i * P:(i + 1) * P], y_t[:, k, :],
                                      start=k == 0, stop=k == KB - 1)
                t.then_inc(s["pj_ps"], 1)
                yield "lg"
                take_mp("lg", m)
                pe.wait_ge(s["t_lo"], m * KB + KB)
                for j in range(B):
                    for k in range(KB):
                        h0 = j * H + k * (P // HD)
                        for i, part in enumerate((t_hi, t_lo)):
                            t = te.matmul(mlog[:, h0:h0 + P // HD, :].rearrange("p h e -> p (h e)"),
                                          part[:, k, j * P:(j + 1) * P].bitcast(F32),
                                          embs[:, :, :].rearrange("p h e -> p (h e)"),
                                          start=i == 0, stop=i == 1)
                t.then_inc(s["lg_ps"], 1)

            def combine(m, c):
                pe.wait_ge(s["acc_ok"], START["acc_ok"] + m * NP * 3 + 6 * c + 6)
                for i in range(4):
                    t = te.matmul(rp[HD * i:HD * i + HD, c, :], stack[:, :], acc[:, i // 2, i % 2, :],
                                  start=True, stop=True)
                t.then_inc(s["cm_ps"], 1)

            def experts(m):
                def take_hp(turn):
                    pe.wait_ge(s["hp_ok"], START["hp_ok"] + m * UNITS * TURNS + max(turn - 1, 0))
                    return hp[turn % 2]

                def layer1(u, c):
                    q, e = u // NG, EG * (u % NG) + c
                    slot = take_hp(TURNS * u + c)
                    for k in range(2):
                        t = te.matmul(slot[:, k, :], w1s[:, e, :], ts[:, 2 * q + k, :], start=True, stop=True)
                    t.then_inc(s["l1_ps"], 1)

                def spread_weights(u):
                    slot = take_hp(TURNS * u + EG)
                    for i in range(2):
                        t = te.matmul(slot[:, i, :], pick[:, i, u % NG, :], wt[:, u // NG, :], start=True, stop=True)
                    t.then_inc(s["wb_ps"], 1)

                yield "l0"
                pe.wait_ge(s["ts_ok"], (m + 1) * SPREAD)
                layer1(0, 0)
                layer1(0, 1)
                yield "wt"
                take_mp("wt", m)
                pe.wait_ge(s["route"], m * ROUTE + ROUTE)
                for q in range(NP):
                    for j in range(B):
                        v = wb[:, j * H + 2 * q:j * H + 2 * q + 2, :, :].rearrange("p h r e -> p (h r e)")
                        t = te.transpose(mwt[:, q, j * P:(j + 1) * P], v, identb[:, :])
                t.then_inc(s["wt_ps"], 1)
                yield "l1"
                layer1(0, 2)
                layer1(0, 3)
                pe.wait_ge(s["wt_ok"], m + 1)
                spread_weights(0)

                for u in range(UNITS):
                    q, gg = u // NG, u % NG
                    yield f"u{u}a"
                    if u + 1 < UNITS:
                        layer1(u + 1, 0)
                        yield f"u{u}b"
                        layer1(u + 1, 1)
                    yield f"u{u}c"
                    pe.wait_ge(s["hp_ok"], START["hp_ok"] + (m * UNITS + u) * TURNS + EG)
                    if u:
                        pe.wait_ge(s["c_ok"], m * UNITS + u)
                    else:
                        pe.wait_ge(s["fin"], START["fin"] + m)
                    if u == 10:
                        pe.wait_ge(s["cm_ok"], START["cm_ok"] + m * 2 + 1)
                    for i in range(2):
                        for j in range(EG):
                            t = te.matmul(rp[HD * j:HD * j + HD, i, :], w2[:, EG * gg + j, :],
                                          g[:, (EG * u + j) % GS, i, :], start=True, stop=True)
                    t.then_inc(s["l2_ps"], 1)
                    if u + 1 < UNITS:
                        yield f"u{u}d"
                        layer1(u + 1, 2)
                        yield f"u{u}e"
                        layer1(u + 1, 3)
                        spread_weights(u + 1)
                    if u == 9:
                        yield "cb0"
                        pe.wait_ge(s["c_ok"], m * UNITS + u + 1)
                        combine(m, 0)

            def tail(m):
                yield "cb1"
                pe.wait_ge(s["c_ok"], m * UNITS + UNITS)
                combine(m, 1)
                yield "out"
                pe.wait_ge(s["cm_ok"], START["cm_ok"] + m * 2 + 2)
                for j in range(B):
                    for k in range(KB):
                        t = te.matmul(otok[:, j, :], comb[:, k, j * P:(j + 1) * P], fo[:, k, :],
                                      start=k == 0, stop=k == KB - 1)
                t.then_inc(s["o_ps"], 1)

            def mp_last(n):
                label = [l for l in MERGED if l in READ_OUT][-1]
                mp_user[0] = (label, n - 1 if label in MIX else n - 2 if label in CHANNEL else n - 3)

            run(MERGED, mix(0, first=True))
            run(MERGED, mix(1), channel(0, first=True))
            run(MERGED, mix(2), channel(1), experts(0))
            with pe.Fori(3, NCH) as n:
                mp_last(n)
                run(MERGED, mix(n), channel(n - 1), experts(n - 2), tail(n - 3))
            mp_last(NCH)
            run(MERGED, channel(NCH - 1), experts(NCH - 2), tail(NCH - 3))
            run(MERGED, experts(NCH - 1), tail(NCH - 2))
            run(MERGED, tail(NCH - 1))


_INS = ["L0_attn_" + n for n in ("x ln1_s ln1_b ln2_s ln2_b tmk tmv tmr w_decay u_first Wk Wv Wr Wo f_tmk f_tmr "
                                 "fWk fWr fWv").split()] + \
       ["L0_ffn_" + n for n in "Wm bm expert_emb W1 b1 W2 b2 Wo bo".split()]


def kernel(**inputs):
    import numpy as _np
    import concourse.bacc as _bacc
    from concourse.bass_utils import run_bass_kernel_spmd as _run

    nc = _bacc.Bacc("TRN2", target_bir_lowering=False, num_devices=1)
    arrays, args = {}, {}
    for name in _INS:
        arr = _np.ascontiguousarray(inputs[name])
        arrays[f"in_{name}"] = arr
        args[name] = nc.dram_tensor(f"in_{name}", arr.shape, mybir.dt.from_np(arr.dtype), kind="ExternalInput").ap()
    shape = inputs["L0_attn_x"].shape
    out = nc.dram_tensor("out", shape, F32, kind="ExternalOutput").ap()
    build(nc, args, out)
    r = _run(nc, [arrays], core_ids=[0])
    return r.results[0]["out"]
```
